# Optimizing a Trainium2 kernel written in Bass

```python
import numpy as np
import jax
import jax.numpy as jnp

def _softmax(x, axis=-1):
    return jax.nn.softmax(x, axis=axis)
def _gelu(x):
    return jax.nn.gelu(x, approximate=True)
def _silu(x):
    return jax.nn.silu(x)
def _sigmoid(x):
    return jax.nn.sigmoid(x)
def _layernorm(x, axis=-1, eps=1e-5):
    m = jnp.mean(x, axis=axis, keepdims=True)
    v = jnp.var(x, axis=axis, keepdims=True)
    return (x - m) / jnp.sqrt(v + eps)
def _scatter_add(tgt, idx, src, axis=0):
    return tgt.at[idx].add(src)
def _segment_sum(src, seg, n):
    return jax.ops.segment_sum(src, seg, n)

kernel_name = 'mk_conv_preact_d1_conv_nchw256_d2cb5a'

def setup_inputs(seed: int = 0):
    np.random.seed(seed)
    _w = jnp.asarray
    def _rec_inputs():
        import jax
        import jax.numpy as jnp
        _gk = jax.random.key(seed)
        x = -0.0003957 + 1 * jax.random.normal(jax.random.fold_in(_gk, 1), (16, 256, 56, 56), jnp.float32)
        return x
    x = _rec_inputs()
    def _L0_conv_setup():
        import jax, jax.numpy as jnp
        import numpy as np
        DIM, K, B, H, W = (256, 7, 16, 56, 56)
        EPS = 1e-05

        def _conv(x, w, pad, groups=1):
            return jax.lax.conv_general_dilated(x, w, window_strides=(1, 1), padding=[(pad, pad), (pad, pad)], dimension_numbers=('NCHW', 'OIHW', 'NCHW'), feature_group_count=groups)

        def _bn(x, g, b, m, v):
            scale = g / jnp.sqrt(v + EPS)
            bias = b - m * scale
            return x * scale[None, :, None, None] + bias[None, :, None, None]

        def _silu(x):
            return x * jax.nn.sigmoid(x)
        key = jax.random.key(seed)
        ks = jax.random.split(key, 12)
        f = lambda k_, shp, s=0.05: jax.random.normal(k_, shp, jnp.float32) * s
        d = {'x': jax.random.normal(ks[0], (B, DIM, H, W), jnp.float32), 'w3': f(ks[1], (DIM, DIM, 3, 3)), 'g1': 1.0 + f(ks[2], (DIM,)), 'b1': f(ks[3], (DIM,)), 'm1': f(ks[4], (DIM,)), 'v1': jax.random.uniform(ks[4], (DIM,), jnp.float32) + 0.5, 'w1': f(ks[5], (DIM, DIM, 1, 1)), 'g2': 1.0 + f(ks[6], (DIM,)), 'b2': f(ks[7], (DIM,)), 'm2': f(ks[8], (DIM,)), 'v2': jax.random.uniform(ks[8], (DIM,), jnp.float32) + 0.5, 'dw7': f(ks[9], (DIM, 1, 7, 7)), 'dwk': f(ks[10], (DIM, 1, K, K)), 'g3': 1.0 + f(ks[11], (DIM,)), 'b3': f(ks[11], (DIM,)), 'm3': f(ks[11], (DIM,)), 'v3': jax.random.uniform(ks[11], (DIM,), jnp.float32) + 0.5}
        return d
    _L0_conv_all = _L0_conv_setup()
    _L0_conv_in = {k: v for k, v in _L0_conv_all.items() if k in ('w3', 'g1', 'b1', 'm1', 'v1', 'w1', 'g2', 'b2', 'm2', 'v2', 'dw7', 'dwk', 'g3', 'b3', 'm3', 'v3', )}
    del _L0_conv_all

    return {
        "x": x,
        "L0_conv_w3": _L0_conv_in["w3"],
        "L0_conv_g1": _L0_conv_in["g1"],
        "L0_conv_b1": _L0_conv_in["b1"],
        "L0_conv_m1": _L0_conv_in["m1"],
        "L0_conv_v1": _L0_conv_in["v1"],
        "L0_conv_w1": _L0_conv_in["w1"],
        "L0_conv_g2": _L0_conv_in["g2"],
        "L0_conv_b2": _L0_conv_in["b2"],
        "L0_conv_m2": _L0_conv_in["m2"],
        "L0_conv_v2": _L0_conv_in["v2"],
        "L0_conv_dw7": _L0_conv_in["dw7"],
        "L0_conv_dwk": _L0_conv_in["dwk"],
        "L0_conv_g3": _L0_conv_in["g3"],
        "L0_conv_b3": _L0_conv_in["b3"],
        "L0_conv_m3": _L0_conv_in["m3"],
        "L0_conv_v3": _L0_conv_in["v3"],
    }

def reference(x, L0_conv_w3, L0_conv_g1, L0_conv_b1, L0_conv_m1, L0_conv_v1, L0_conv_w1, L0_conv_g2, L0_conv_b2, L0_conv_m2, L0_conv_v2, L0_conv_dw7, L0_conv_dwk, L0_conv_g3, L0_conv_b3, L0_conv_m3, L0_conv_v3):
    import jax
    import jax.numpy as jnp
    def _L0_conv_ref(x, w3, g1, b1, m1, v1, w1, g2, b2, m2, v2, dw7, dwk, g3, b3, m3, v3):
        import jax, jax.numpy as jnp
        import numpy as np
        DIM, K, B, H, W = (256, 7, 16, 56, 56)
        EPS = 1e-05

        def _conv(x, w, pad, groups=1):
            return jax.lax.conv_general_dilated(x, w, window_strides=(1, 1), padding=[(pad, pad), (pad, pad)], dimension_numbers=('NCHW', 'OIHW', 'NCHW'), feature_group_count=groups)

        def _bn(x, g, b, m, v):
            scale = g / jnp.sqrt(v + EPS)
            bias = b - m * scale
            return x * scale[None, :, None, None] + bias[None, :, None, None]

        def _silu(x):
            return x * jax.nn.sigmoid(x)
        rep = _silu(_bn(_conv(x, w3, 1), g1, b1, m1, v1) + _bn(_conv(x, w1, 0), g2, b2, m2, v2))
        y = rep + _conv(x, dw7, 3, groups=DIM) + _conv(x, dwk, K // 2, groups=DIM)
        return _silu(_bn(y, g3, b3, m3, v3))

    def _gn(v, G=32, eps=1e-5):
        B_, C_, H_, W_ = v.shape
        g = v.reshape(B_, G, C_ // G, H_, W_)
        m = jnp.mean(g, axis=(2, 3, 4), keepdims=True)
        s = jnp.var(g, axis=(2, 3, 4), keepdims=True)
        return ((g - m) / jnp.sqrt(s + eps)).reshape(v.shape)

    def _ln_c(v, eps=1e-6):
        m = jnp.mean(v, axis=1, keepdims=True)
        s = jnp.var(v, axis=1, keepdims=True)
        return (v - m) / jnp.sqrt(s + eps)

    def _ln_t(v, eps=1e-5):
        m = jnp.mean(v, axis=-1, keepdims=True)
        s = jnp.var(v, axis=-1, keepdims=True)
        return (v - m) / jnp.sqrt(s + eps)

    def _to_tokens(v):
        B_, C_, H_, W_ = v.shape
        return v.reshape(B_, C_, H_ * W_).transpose(0, 2, 1)
    def _from_tokens(t, like):
        B_, C_, H_, W_ = like.shape
        return t.transpose(0, 2, 1).reshape(B_, C_, H_, W_)

    x = x + _L0_conv_ref(_gn(x), L0_conv_w3, L0_conv_g1, L0_conv_b1, L0_conv_m1, L0_conv_v1, L0_conv_w1, L0_conv_g2, L0_conv_b2, L0_conv_m2, L0_conv_v2, L0_conv_dw7, L0_conv_dwk, L0_conv_g3, L0_conv_b3, L0_conv_m3, L0_conv_v3)
    return x


_drawn_inputs = setup_inputs


def setup_inputs(seed=0):
    import zlib

    import numpy as np

    out = dict(_drawn_inputs(seed))
    spreads = {}
    factors = {'L0_conv_b1': 3.752,
     'L0_conv_m1': 3.216,
     'L0_conv_g2': 3.666,
     'L0_conv_b2': 3.26,
     'L0_conv_m2': 3.269,
     'L0_conv_b3': 3.17,
     'L0_conv_m3': 3.018}
    for name, (base, spread) in spreads.items():
        noise = np.random.default_rng([zlib.crc32(name.encode()), seed]).standard_normal(out[name].shape)
        drawn = base * np.exp(spread * noise) if base else spread * noise
        out[name] = jnp.asarray(drawn.astype(out[name].dtype))
    for name, factor in factors.items():
        out[name] = (out[name] * factor).astype(out[name].dtype)
    return out
```

```python
from contextlib import ExitStack

import numpy as np
import concourse.bass as bass
from concourse import mybir

F32 = mybir.dt.float32
F16 = mybir.dt.float16
ALU = mybir.AluOpType
ACT = mybir.ActivationFunctionType
AXX = mybir.AxisListType.X

P = 128
B, C, H, W = 16, 256, 56, 56
HW = H * W
CT = C // P
GROUP_C = C // 32
GN_EPS = 1e-5
BN_EPS = 1e-5
XS = 128.0
WS = 256.0

K7 = 7
R7 = K7 // 2
PITCH = W + R7
REACH = R7 * PITCH + R7
OUT_BLOCKS = -(-(PITCH * (H - 1) + W) // P)
TAP_BLOCKS = 4
LEAD = REACH - P
IN_BLOCKS = OUT_BLOCKS + 1
STRIP = TAP_BLOCKS * P
VEC = STRIP + P
CC = 16
CHUNKS = C // CC
BH = B // 2
SG = 4
SGROUPS = CC // SG
IN_BATCHES = -(-IN_BLOCKS // 4)
HALF_BLOCKS = OUT_BLOCKS // 2

KW = 4
WPAD = W + 2
STEP_ROWS = H // 2
PAIRS = STEP_ROWS // 2
TPAIRS = PAIRS // 2
N3 = TPAIRS * W
TROWS = 2 * TPAIRS


def strip_centre():
    return P + LEAD + P - 1


def build(nc, x, w3, g1, b1, m1, v1, w1, g2, b2, m2, v2, dw7, dwk, g3, b3, m3, v3, ident_d, gmat_d, out):
    root = ExitStack()

    def sb(ctx, name, shape, dt=F32):
        return ctx.enter_context(nc.sbuf_tensor(name, shape, dt))

    def sem(name):
        return root.enter_context(nc.semaphore(name))

    x3 = x.rearrange("b c h w -> b c (h w)")
    out3 = out.rearrange("b c h w -> b c (h w)")
    vec_d = nc.dram_tensor("strip_vectors", [C, 2, VEC], F16, kind="Internal").ap()
    dw_d = nc.dram_tensor("depthwise_out", [B, C, OUT_BLOCKS * P], F32, kind="Internal").ap()
    st_d = nc.dram_tensor("gn_stats", [C, B, 2], F32, kind="Internal").ap()

    with root:
        bank = [root.enter_context(nc.psum_tensor(f"bank{i}", [P, 512], F32)) for i in range(8)]
        ident = sb(root, "ident", [P, P])
        fold3 = sb(root, "fold3", [P, CT])
        bias3 = sb(root, "bias3", [P, CT])
        dw_scale = sb(root, "dw_scale", [P, CT])
        eps_bn = sb(root, "eps_bn", [P, 1])

        with ExitStack() as ctx:
            dwa = sb(ctx, "dwa", [P, CT, K7 * K7])
            dwb = sb(ctx, "dwb", [P, CT, K7 * K7])
            dmax = sb(ctx, "dmax", [P, CT])
            dmin = sb(ctx, "dmin", [P, CT])
            dinv = sb(ctx, "dinv", [P, CT])
            vec = sb(ctx, "vec", [P, CT, VEC])
            vech = sb(ctx, "vech", [P, CT, 2, VEC], F16)
            p3 = sb(ctx, "p3", [P, 4, CT])
            std3 = sb(ctx, "std3", [P, CT])
            s_dw, s_p3, s_id, s_vd, s_st3, s_vout = (sem(n) for n in
                ("dw_loaded", "p3_loaded", "ident_loaded", "filter_steps", "std3_ready", "vectors_stored"))

            block = ctx.enter_context(nc.Block())

            @block.sync
            def _(sp):
                with nc.allow_non_contiguous_dma(reason="one value per channel"):
                    sp.dma_start(dwa[:], dw7.rearrange("(k p) o y x -> p k (o y x)", p=P)).then_inc(s_dw, 16)
                    sp.dma_start(dwb[:], dwk.rearrange("(k p) o y x -> p k (o y x)", p=P)).then_inc(s_dw, 16)
                    for n, a in enumerate((g3, b3, m3, v3)):
                        sp.dma_start(p3[:, n, :], a.rearrange("(k p) -> p k", p=P)).then_inc(s_p3, 16)
                sp.dma_start(ident[:], ident_d).then_inc(s_id, 16)
                sp.wait_ge(s_id, 16)
                sp.wait_ge(s_vd, 13)
                for k in range(CT):
                    sp.dma_start(vec_d[k * P:(k + 1) * P], vech[:, k]).then_inc(s_vout, 16)
                sp.wait_ge(s_vout, 16 * CT)

            @block.scalar
            def _(act):
                act.wait_ge(s_p3, 64)
                act.wait_ge(s_vd, 1)
                nc.scalar.activation(std3[:], p3[:, 3, :], ACT.Sqrt, bias=eps_bn[:, 0:1]).then_inc(s_st3, 1)

            @block.vector
            def _(dve):
                nc.vector.memset(eps_bn[:], BN_EPS).then_inc(s_vd, 1)
                nc.vector.memset(vec[:], 0.0).then_inc(s_vd, 1)
                dve.wait_ge(s_dw, 32)
                nc.vector.tensor_tensor(dwa[:], dwa[:], dwb[:], ALU.add).then_inc(s_vd, 1)
                dve.wait_ge(s_vd, 3)
                nc.vector.tensor_reduce(dmax[:], dwa[:], AXX, ALU.max).then_inc(s_vd, 1)
                nc.vector.tensor_reduce(dmin[:], dwa[:], AXX, ALU.min).then_inc(s_vd, 1)
                dve.wait_ge(s_vd, 5)
                nc.vector.scalar_tensor_tensor(dmax[:], dmin[:], -1.0, dmax[:], ALU.mult, ALU.max).then_inc(s_vd, 1)
                dve.wait_ge(s_vd, 6)
                nc.vector.tensor_scalar(dmax[:], dmax[:], 1e-30, None, ALU.max).then_inc(s_vd, 1)
                dve.wait_ge(s_vd, 7)
                nc.vector.reciprocal(dinv[:], dmax[:]).then_inc(s_vd, 1)
                nc.vector.tensor_scalar(dw_scale[:], dmax[:], 1.0 / (WS * XS), None, ALU.mult).then_inc(s_vd, 1)
                dve.wait_ge(s_vd, 8)
                at = strip_centre() - REACH
                for k in range(CT):
                    rows = vec[:, k, at:at + K7 * PITCH].rearrange("p (y x) -> p y x", x=PITCH)[:, :, 0:K7]
                    nc.vector.tensor_scalar(rows, dwa[:, k, :].rearrange("p (y x) -> p y x", x=K7),
                                            dinv[:, k:k + 1], WS, ALU.mult, ALU.mult).then_inc(s_vd, 1)
                dve.wait_ge(s_vd, 11)
                nc.vector.tensor_copy(vech[:, :, 0, :], vec[:]).then_inc(s_vd, 1)
                dve.wait_ge(s_vd, 12)
                nc.vector.tensor_tensor(vech[:, :, 1, :], vec[:], vech[:, :, 0, :], ALU.subtract).then_inc(s_vd, 1)
                dve.wait_ge(s_st3, 1)
                nc.vector.reciprocal(std3[:], std3[:]).then_inc(s_vd, 1)
                dve.wait_ge(s_vd, 14)
                nc.vector.tensor_tensor(fold3[:], std3[:], p3[:, 0, :], ALU.mult).then_inc(s_vd, 1)
                dve.wait_ge(s_vd, 15)
                nc.vector.tensor_tensor(p3[:, 2, :], p3[:, 2, :], fold3[:], ALU.mult).then_inc(s_vd, 1)
                dve.wait_ge(s_vd, 16)
                nc.vector.tensor_tensor(bias3[:], p3[:, 1, :], p3[:, 2, :], ALU.subtract).then_inc(s_vd, 1)

        depthwise(nc, root, sb, sem, bank, ident, x3, vec_d, dw_d, st_d, gmat_d)

        with ExitStack() as ctx:
            wt = sb(ctx, "wt", [P, CT, KW, 3, 2, C], F16)
            scale1 = sb(ctx, "scale1", [P, CT])
            bias1 = sb(ctx, "bias1", [P, CT])
            stats = sb(ctx, "stats", [P, CT, B, 2])
            dense_weights(nc, sb, sem, bank, ident, eps_bn, wt, scale1, bias1, stats, st_d,
                          w3, w1, (g1, b1, m1, v1), (g2, b2, m2, v2))
            dense(nc, ctx, sb, sem, bank, wt, scale1, bias1, stats, fold3, bias3, dw_scale, x3, dw_d, out3)
    return nc


def depthwise(nc, root, sb, sem, bank, ident, x3, vec_d, dw_d, st_d, gmat_d):
    T, CV, BK, GS = bank[0:2], bank[2:6], bank[6], bank[7]
    with ExitStack() as ctx:
        gmat = sb(ctx, "gmat", [P, P])
        eps_gn = sb(ctx, "eps_gn", [P, 1])
        Xa = [sb(ctx, f"Xa{h}", [P, HW]) for h in range(2)]
        Xp = [sb(ctx, f"Xp{h}", [P, IN_BLOCKS * P]) for h in range(2)]
        D = [sb(ctx, f"D{s}", [P, 2, CC, IN_BLOCKS * B], F16) for s in range(2)]
        S = [sb(ctx, f"S{g}", [P, SG, 2, STRIP], F16) for g in range(SGROUPS)]
        Y = [sb(ctx, f"Y{s}", [P, 2, OUT_BLOCKS, CC * BH]) for s in range(2)]
        O = [sb(ctx, f"O{q}", [P, HALF_BLOCKS * P]) for q in range(2)]
        bn = [sb(ctx, f"bn{h}", [P, 7, 6]) for h in range(2)]
        mv = [sb(ctx, f"mv{h}", [P, 2]) for h in range(2)]
        dev = [sb(ctx, f"dev{h}", [P, 2]) for h in range(2)]
        std = [sb(ctx, f"std{h}", [P, 1]) for h in range(2)]
        st = [[sb(ctx, f"st{s}{h}", [P, 2]) for h in range(2)] for s in range(2)]

        s_const, s_zero = sem("gmat_loaded"), sem("padding_zeroed")
        xa_loaded = [sem(f"xa_loaded{h}") for h in range(2)]
        xp_ready = [sem(f"xp_ready{h}") for h in range(2)]
        t_full = [sem(f"t_full{i}") for i in range(2)]
        t_high = [sem(f"t_high{i}") for i in range(2)]
        t_low = [sem(f"t_low{i}") for i in range(2)]
        s_loaded = [sem(f"s_loaded{g}") for g in range(SGROUPS)]
        cv_full = [sem(f"cv_full{i}") for i in range(4)]
        cv_free = [sem(f"cv_free{i}") for i in range(4)]
        bk_full, bk_free = sem("bk_full"), sem("bk_free")
        o_stored = [sem(f"o_stored{q}") for q in range(2)]
        st_stored = [sem(f"st_stored{s}") for s in range(2)]
        q_pieces = [sem(f"bn_pieces{h}") for h in range(2)]
        q_aggr = [sem(f"bn_aggr{h}") for h in range(2)]
        q_gmean = [sem(f"group_mean{h}") for h in range(2)]
        q_diff = [sem(f"mean_diff{h}") for h in range(2)]
        q_dev = [sem(f"deviation{h}") for h in range(2)]
        q_gvar = [sem(f"group_var{h}") for h in range(2)]
        q_std = [sem(f"group_std{h}") for h in range(2)]
        q_rstd = [sem(f"group_rstd{h}") for h in range(2)]

        def chunks(eng, step):
            step(0, 0, 0)
            with eng.Fori(0, (CHUNKS - 4) // 2) as i:
                step(i * 2 + 1, i, 1)
                step(i * 2 + 2, i + 1, 0)
            step(CHUNKS - 3, (CHUNKS - 3) // 2, 1)
            step(CHUNKS - 2, (CHUNKS - 2) // 2, 0)
            step(CHUNKS - 1, (CHUNKS - 1) // 2, 1)

        def has(n, last):
            return not isinstance(n, int) or n <= last

        def in_blocks(k):
            return range(4 * k, min(4 * k + 4, IN_BLOCKS))

        IN_SLOTS = [(h, k) for h in range(2) for k in range(IN_BATCHES)]
        OUT_SLOTS = [(h, q, range(4 * k, min(4 * k + 4, HALF_BLOCKS))) for h in range(2) for q in range(2)
                     for k in range(4)]

        block = ctx.enter_context(nc.Block())

        @block.gpsimd
        def _(pool):
            for h in range(2):
                nc.gpsimd.memset(Xp[h][:], 0.0).then_inc(s_zero, 1)
            nc.gpsimd.memset(eps_gn[:], GN_EPS / (XS * XS)).then_inc(s_zero, 1)
            with pool.Fori(0, CHUNKS) as n:
                for h in range(2):
                    pool.wait_ge(xp_ready[h], n)
                    src = x3[h * BH:(h + 1) * BH, bass.ds(n * CC, CC), :].rearrange("b c q -> c b q")
                    pool.dma_start(Xa[h][:], src).then_inc(xa_loaded[h], 16)

        @block.sync
        def _(sp):
            sp.dma_start(gmat[:], gmat_d).then_inc(s_const, 16)

            def load_strips(n, g):
                v = vec_d[bass.ds(n * CC + g * SG, SG)]
                src = bass.AP(v.tensor, v.offset, [[1, P], [VEC, SG * 2], [1, STRIP]])
                sp.dma_start(S[g][:].rearrange("p c z m -> p (c z) m"), src).then_inc(s_loaded[g], 16)

            def store_stats(n, m, s):
                for h in range(2):
                    sp.wait_ge(q_rstd[h], n + 1)
                    dst = st_d[bass.ds(n * CC, CC), h * BH:(h + 1) * BH, :]
                    sp.dma_start(dst, st[s][h][:]).then_inc(st_stored[s], 16)

            def store_out(n, p):
                h, q = p // 2, p % 2
                sp.wait_ge(bk_free, n * 16 + 4 * p + 4)
                dst = dw_d[h * BH:(h + 1) * BH, bass.ds(n * CC, CC),
                           q * HALF_BLOCKS * P:(q + 1) * HALF_BLOCKS * P].rearrange("b c q -> c b q")
                sp.dma_start(dst, O[q][:]).then_inc(o_stored[q], 16)

            for g in range(SGROUPS):
                load_strips(0, g)
            store_stats(0, 0, 0)
            store_stats(1, 0, 1)

            def step(n, m, s):
                for g in range(SGROUPS):
                    if has(n, CHUNKS - 2):
                        sp.wait_ge(cv_full[SG - 1], n * SGROUPS + g + 1)
                        load_strips(n + 1, g)
                    if not (isinstance(n, int) and n == 0):
                        store_out(n - 1, g)
                if has(n, CHUNKS - 3):
                    store_stats(n + 2, m + 1, s)

            chunks(sp, step)
            for p in range(4):
                store_out(CHUNKS - 1, p)
            for q in range(2):
                sp.wait_ge(o_stored[q], 16 * 2 * CHUNKS)
            for s in range(2):
                sp.wait_ge(st_stored[s], 16 * CHUNKS)

        @block.tensor
        def _(pe):
            def group_mean(n, h):
                pe.wait_ge(q_std[1 - h], n + h)
                pe.wait_ge(q_aggr[h], n + 1)
                nc.tensor.matmul(GS[:, 2 * h:2 * h + 1], gmat[:], mv[h][:, 0:1], start=True, stop=True
                                 ).then_inc(q_gmean[h], 1)

            def group_var(n, h):
                pe.wait_ge(q_dev[h], n + 1)
                nc.tensor.matmul(GS[:, 2 * h + 1:2 * h + 2], gmat[:], dev[h][:, 1:2], start=True, stop=True
                                 ).then_inc(q_gvar[h], 1)

            def transpose_in(n, slot):
                h, k = IN_SLOTS[slot]
                if k == 0:
                    pe.wait_ge(xp_ready[h], n + 1)
                pe.wait_ge(t_low[slot % 2], n * 7 + slot // 2)
                for j, b in enumerate(in_blocks(k)):
                    last = nc.tensor.transpose(T[slot % 2][:, j * P:(j + 1) * P],
                                               Xp[h][:, b * P:(b + 1) * P], ident[:])
                last.then_inc(t_full[slot % 2], 1)

            def transpose_out(n, s, slot):
                h, q, blocks = OUT_SLOTS[slot]
                if slot == 0:
                    for i in range(4):
                        pe.wait_ge(cv_free[i], (n + 1) * 4)
                pe.wait_ge(bk_free, n * 16 + slot)
                for j, b in enumerate(blocks):
                    last = nc.tensor.transpose(BK[:, j * P:(j + 1) * P],
                                               Y[s][:, h, q * HALF_BLOCKS + b, :], ident[:])
                last.then_inc(bk_full, 1)

            def convolve(n, s, c):
                if c == 0:
                    for i in range(2):
                        pe.wait_ge(t_low[i], (n + 1) * 7)
                if c % SG == 0:
                    pe.wait_ge(s_loaded[c // SG], (n + 1) * 16)
                pe.wait_ge(cv_free[c % 4], n * 4 + c // 4)
                strip, data, acc = S[c // SG], D[s], CV[c % 4]
                n_out = OUT_BLOCKS * B
                for z, (hs, hd) in enumerate(((0, 0), (0, 1), (1, 0))):
                    for j in (1, 2, 0, 3):
                        lo = B if j == 0 else 0
                        hi = n_out - B if j == 3 else n_out
                        last = nc.tensor.matmul(
                            acc[:, lo:hi], strip[:, c % SG, hs, j * P:(j + 1) * P],
                            data[:, hd, c, lo + (j - 1) * B:hi + (j - 1) * B],
                            start=(z == 0 and j == 1), stop=(z == 2 and j == 3))
                last.then_inc(cv_full[c % 4], 1)

            pe.wait_ge(s_const, 16)
            for n in range(2):
                for h in range(2):
                    group_mean(n, h)
                    group_var(n, h)
                if n == 0:
                    for slot in range(len(IN_SLOTS)):
                        transpose_in(0, slot)

            def step(n, m, s):
                first = isinstance(n, int) and n == 0
                for c in range(CC):
                    convolve(n, s, c)
                    if not first:
                        transpose_out(n - 1, 1 - s, c)
                    if c < len(IN_SLOTS) and has(n, CHUNKS - 2):
                        transpose_in(n + 1, c)
                    if has(n, CHUNKS - 3):
                        if c in (5, 9):
                            group_mean(n + 2, c // 4 - 1)
                        if c in (7, 11):
                            group_var(n + 2, c // 4 - 1)

            chunks(pe, step)
            for slot in range(CC):
                transpose_out(CHUNKS - 1, 1, slot)

        @block.scalar
        def _(act):
            def take_high(n, s, slot):
                h, k = IN_SLOTS[slot]
                nb = len(in_blocks(k))
                act.wait_ge(t_full[slot % 2], n * 7 + slot // 2 + 1)
                dst = D[s][:, 0].rearrange("p c (k b) -> p k c b", b=B)[:, 4 * k:4 * k + nb, :, h * BH:(h + 1) * BH]
                src = T[slot % 2][:, 0:nb * P].rearrange("p (k c b) -> p k c b", c=CC, b=BH)
                nc.scalar.copy(dst, src).then_inc(t_high[slot % 2], 1)

            def take_conv(n, s, c):
                act.wait_ge(cv_full[c % 4], n * 4 + c // 4 + 1)
                dst = Y[s][:, :, :, c * BH:(c + 1) * BH].rearrange("p h k b -> p k h b")
                src = CV[c % 4][:, 0:OUT_BLOCKS * B].rearrange("p (k h b) -> p k h b", h=2, b=BH)
                nc.scalar.copy(dst, src).then_inc(cv_free[c % 4], 1)

            def take_out(n, slot):
                h, q, blocks = OUT_SLOTS[slot]
                if slot % 4 == 0 and not (isinstance(n, int) and n == 0 and h == 0):
                    act.wait_ge(o_stored[q], (n * 2 + h) * 16)
                act.wait_ge(bk_full, n * 16 + slot + 1)
                dst = O[q][:, blocks[0] * P:(blocks[-1] + 1) * P].rearrange("p (k m) -> p k m", m=P)
                src = BK[:, 0:len(blocks) * P].rearrange("p (k m) -> p k m", m=P)
                nc.scalar.copy(dst, src[:, :, ::-1]).then_inc(bk_free, 1)

            def group_std(n, h):
                act.wait_ge(q_gvar[h], n + 1)
                nc.scalar.activation(std[h][:], GS[:, 2 * h + 1:2 * h + 2], ACT.Sqrt, bias=eps_gn[:, 0:1],
                                     scale=1.0 / (XS * XS)).then_inc(q_std[h], 1)

            act.wait_ge(s_zero, 3)
            for n in range(2):
                for h in range(2):
                    group_std(n, h)
                if n == 0:
                    for slot in range(len(IN_SLOTS)):
                        take_high(0, 0, slot)

            def step(n, m, s):
                first = isinstance(n, int) and n == 0
                for c in range(CC):
                    if c in (8, 12) and has(n, CHUNKS - 3):
                        group_std(n + 2, c // 4 - 2)
                    take_conv(n, s, c)
                    if not first:
                        take_out(n - 1, c)
                    if c < len(IN_SLOTS) and has(n, CHUNKS - 2):
                        take_high(n + 1, 1 - s, c)


            chunks(act, step)
            for slot in range(CC):
                take_out(CHUNKS - 1, slot)

        @block.vector
        def _(dve):
            def stat_piece(n, h, k):
                if k == 0:
                    dve.wait_ge(xa_loaded[h], (n + 1) * 16)
                nc.vector.bn_stats(bn[h][:, k, :], Xa[h][:, k * 448:(k + 1) * 448]).then_inc(q_pieces[h], 1)

            def stat_pieces_done(n, h):
                dve.wait_ge(q_pieces[h], (n + 1) * 7)

            def stat_aggregate(n, h):
                nc.vector.bn_aggr(mv[h][:], bn[h][:].rearrange("p k v -> p (k v)")).then_inc(q_aggr[h], 1)

            def stat_deviation(n, m, s, h):
                dve.wait_ge(q_gmean[h], n + 1)
                dve.wait_ge(st_stored[s], m * 32)
                nc.vector.tensor_copy(st[s][h][:, 0:1], GS[:, 2 * h:2 * h + 1])
                nc.vector.tensor_tensor(dev[h][:, 0:1], mv[h][:, 0:1], GS[:, 2 * h:2 * h + 1], ALU.subtract
                                        ).then_inc(q_diff[h], 1)
                dve.wait_ge(q_diff[h], n + 1)
                nc.vector.scalar_tensor_tensor(dev[h][:, 1:2], dev[h][:, 0:1], dev[h][:, 0:1], mv[h][:, 1:2],
                                               ALU.mult, ALU.add).then_inc(q_dev[h], 1)

            def normalise(n, s, h):
                dve.wait_ge(q_std[h], n + 1)
                nc.vector.reciprocal(st[s][h][:, 1:2], std[h][:]).then_inc(q_rstd[h], 1)
                dve.wait_ge(q_rstd[h], n + 1)
                slot = IN_BATCHES * (h + 1) - 1
                if not (isinstance(n, int) and n == 0):
                    dve.wait_ge(t_full[slot % 2], n * 7 - 7 + slot // 2 + 1)
                dst = Xp[h][:, LEAD:LEAD + H * PITCH].rearrange("p (y x) -> p y x", x=PITCH)[:, :, 0:W]
                nc.vector.tensor_scalar(dst, Xa[h][:].rearrange("p (y x) -> p y x", x=W), st[s][h][:, 0:1],
                                        st[s][h][:, 1:2], ALU.subtract, ALU.mult).then_inc(xp_ready[h], 1)

            def take_low(n, s, slot):
                h, k = IN_SLOTS[slot]
                nb = len(in_blocks(k))
                dve.wait_ge(t_high[slot % 2], n * 7 + slot // 2 + 1)

                def part(z):
                    return D[s][:, z].rearrange("p c (k b) -> p k c b", b=B)[:, 4 * k:4 * k + nb, :, h * BH:(h + 1) * BH]

                src = T[slot % 2][:, 0:nb * P].rearrange("p (k c b) -> p k c b", c=CC, b=BH)
                nc.vector.tensor_tensor(part(1), src, part(0), ALU.subtract).then_inc(t_low[slot % 2], 1)

            dve.wait_ge(s_zero, 3)
            for n in range(2):
                for h in range(2):
                    for k in range(7):
                        stat_piece(n, h, k)
                    stat_pieces_done(n, h)
                    stat_aggregate(n, h)
                    stat_deviation(n, 0, n, h)
                    if n == 0:
                        normalise(n, n, h)
                if n == 0:
                    for slot in range(len(IN_SLOTS)):
                        take_low(0, 0, slot)
            for h in range(2):
                normalise(1, 1, h)

            def step(n, m, s):
                for c in range(CC):
                    if c in (4, 8) and has(n, CHUNKS - 3):
                        stat_pieces_done(n + 2, c // 4 - 1)
                    if c < len(IN_SLOTS) and has(n, CHUNKS - 2):
                        take_low(n + 1, 1 - s, c)
                    if has(n, CHUNKS - 3):
                        for h in range(2):
                            k = c - 4 * h
                            if 0 <= k < 4:
                                for piece in range(2 * k, min(2 * k + 2, 7)):
                                    stat_piece(n + 2, h, piece)
                            if k == 4:
                                stat_aggregate(n + 2, h)
                            if k == 6:
                                stat_deviation(n + 2, m + 1, s, h)
                        if c in (9, 14):
                            normalise(n + 2, s, c // 14)

            chunks(dve, step)


def dense_weights(nc, sb, sem, bank, ident, eps_bn, wt, scale1, bias1, stats, st_d, w3, w1, bn1, bn2):
    with ExitStack() as ctx:
        wn = sb(ctx, "wn", [P, CT, C, 9])
        wc = sb(ctx, "wc", [P, CT, C])
        wk = sb(ctx, "wk", [P, CT, KW, 3, C])
        wsum = sb(ctx, "wsum", [P, CT, 3, C])
        pn = sb(ctx, "pn", [P, 2, 4, CT])
        sd = sb(ctx, "sd", [P, 2, CT])
        fold = sb(ctx, "fold", [P, 2, CT])
        wmax = sb(ctx, "wmax", [P, CT])
        wmin = sb(ctx, "wmin", [P, CT])
        winv = sb(ctx, "winv", [P, CT])
        s_w, s_pn, s_sts, s_d, s_sq = (sem(n) for n in
            ("w3_loaded", "bn_loaded", "stats_loaded", "weight_steps", "bn_std"))
        s_t = [sem(f"wt_full{i}") for i in range(2)]
        s_hi = [sem(f"wt_high{i}") for i in range(2)]
        s_lo = [sem(f"wt_low{i}") for i in range(2)]
        block = ctx.enter_context(nc.Block())
        BATCHES = [(co, ci, k) for co in range(CT) for ci in range(CT) for k in range(KW)]

        @block.sync
        def _(sp):
            sp.dma_start(wn[:].rearrange("p k i t -> p k (i t)"),
                         w3.rearrange("(k p) i y x -> p k (i y x)", p=P)).then_inc(s_w, 16)
            sp.dma_start(wc[:], w1.rearrange("(k p) i y x -> p k (i y x)", p=P)).then_inc(s_w, 16)
            with nc.allow_non_contiguous_dma(reason="one value per channel"):
                for i, bns in enumerate((bn1, bn2)):
                    for j, a in enumerate(bns):
                        sp.dma_start(pn[:, i, j, :], a.rearrange("(k p) -> p k", p=P)).then_inc(s_pn, 16)
            sp.dma_start(stats[:].rearrange("p k b v -> p k (b v)"),
                         st_d.rearrange("(k p) b v -> p k (b v)", p=P)).then_inc(s_sts, 16)
            sp.wait_ge(s_sts, 16)

        @block.scalar
        def _(act):
            act.wait_ge(s_pn, 128)
            nc.scalar.activation(sd[:], pn[:, :, 3, :], ACT.Sqrt, bias=eps_bn[:, 0:1]).then_inc(s_sq, 1)
            for n, (co, ci, k) in enumerate(BATCHES):
                act.wait_ge(s_t[n % 2], n // 2 + 1)
                nc.scalar.copy(wt[:, ci, k, :, 0, co * P:(co + 1) * P],
                               bank[n % 2][:, 0:3 * P].rearrange("p (d m) -> p d m", m=P)).then_inc(s_hi[n % 2], 1)

        @block.vector
        def _(dve):
            done = 0
            dve.wait_ge(s_sq, 1)
            nc.vector.reciprocal(sd[:], sd[:]).then_inc(s_d, 1)
            dve.wait_ge(s_d, 1)
            nc.vector.tensor_tensor(fold[:], sd[:], pn[:, :, 0, :], ALU.mult).then_inc(s_d, 1)
            dve.wait_ge(s_d, 2)
            nc.vector.tensor_tensor(pn[:, :, 2, :], pn[:, :, 2, :], fold[:], ALU.mult).then_inc(s_d, 1)
            dve.wait_ge(s_d, 3)
            nc.vector.tensor_tensor(pn[:, :, 1, :], pn[:, :, 1, :], pn[:, :, 2, :], ALU.subtract).then_inc(s_d, 1)
            dve.wait_ge(s_d, 4)
            nc.vector.tensor_tensor(bias1[:], pn[:, 0, 1, :], pn[:, 1, 1, :], ALU.add).then_inc(s_d, 1)
            dve.wait_ge(s_w, 32)
            for k in range(CT):
                nc.vector.tensor_scalar(wn[:, k], wn[:, k], fold[:, 0, k:k + 1], None, ALU.mult).then_inc(s_d, 1)
            dve.wait_ge(s_d, 7)
            for k in range(CT):
                nc.vector.scalar_tensor_tensor(wn[:, k, :, 4], wc[:, k], fold[:, 1, k:k + 1], wn[:, k, :, 4],
                                               ALU.mult, ALU.add).then_inc(s_d, 1)
            dve.wait_ge(s_d, 9)
            flat = wn[:].rearrange("p k i t -> p k (i t)")
            nc.vector.tensor_reduce(wmax[:], flat, AXX, ALU.max).then_inc(s_d, 1)
            nc.vector.tensor_reduce(wmin[:], flat, AXX, ALU.min).then_inc(s_d, 1)
            dve.wait_ge(s_d, 11)
            nc.vector.scalar_tensor_tensor(wmax[:], wmin[:], -1.0, wmax[:], ALU.mult, ALU.max).then_inc(s_d, 1)
            dve.wait_ge(s_d, 12)
            nc.vector.tensor_scalar(wmax[:], wmax[:], 1e-30, None, ALU.max).then_inc(s_d, 1)
            dve.wait_ge(s_d, 13)
            nc.vector.reciprocal(winv[:], wmax[:]).then_inc(s_d, 1)
            nc.vector.tensor_scalar(scale1[:], wmax[:], 1.0 / (WS * XS), None, ALU.mult).then_inc(s_d, 1)
            dve.wait_ge(s_d, 14)
            for k in range(CT):
                taps = wn[:, k].rearrange("p i (y x) -> p y x i", x=3)
                nc.vector.tensor_scalar(wk[:, k, 0], taps[:, 0], winv[:, k:k + 1], WS, ALU.mult, ALU.mult
                                        ).then_inc(s_d, 1)
                nc.vector.tensor_scalar(wk[:, k, 3], taps[:, 2], winv[:, k:k + 1], WS, ALU.mult, ALU.mult
                                        ).then_inc(s_d, 1)
                nc.vector.tensor_scalar(wk[:, k, 1], taps[:, 1], winv[:, k:k + 1], WS / 2, ALU.mult, ALU.mult
                                        ).then_inc(s_d, 1)
                dve.wait_ge(s_d, 15 + 6 * k + 3)
                nc.vector.tensor_tensor(wsum[:, k], wk[:, k, 0], wk[:, k, 3], ALU.add).then_inc(s_d, 1)
                dve.wait_ge(s_d, 15 + 6 * k + 4)
                nc.vector.scalar_tensor_tensor(wk[:, k, 2], wsum[:, k], 0.5, wk[:, k, 1], ALU.mult, ALU.subtract
                                               ).then_inc(s_d, 1)
                dve.wait_ge(s_d, 15 + 6 * k + 5)
                nc.vector.scalar_tensor_tensor(wk[:, k, 1], wsum[:, k], 0.5, wk[:, k, 1], ALU.mult, ALU.add
                                               ).then_inc(s_d, 1)
            for n, (co, ci, k) in enumerate(BATCHES):
                dve.wait_ge(s_hi[n % 2], n // 2 + 1)
                dst = wt[:, ci, k, :, :, co * P:(co + 1) * P]
                nc.vector.tensor_tensor(dst[:, :, 1], bank[n % 2][:, 0:3 * P].rearrange("p (d m) -> p d m", m=P),
                                        dst[:, :, 0], ALU.subtract).then_inc(s_lo[n % 2], 1)

        @block.tensor
        def _(pe):
            for n, (co, ci, k) in enumerate(BATCHES):
                pe.wait_ge(s_d, 15 + 6 * (co + 1))
                if n >= 2:
                    pe.wait_ge(s_lo[n % 2], n // 2)
                for d in range(3):
                    last = nc.tensor.transpose(bank[n % 2][:, d * P:(d + 1) * P],
                                               wk[:, co, k, d, ci * P:(ci + 1) * P], ident[:])
                last.then_inc(s_t[n % 2], 1)


def dense(nc, ctx, sb, sem, bank, wt, scale1, bias1, stats, fold3, bias3, dw_scale, x3, dw_d, out3):
    Xb = [sb(ctx, f"Xb{i}", [P, CT, H, W]) for i in range(2)]
    xn = sb(ctx, "xn", [P, CT, STEP_ROWS + 3, WPAD])
    U = [sb(ctx, f"U{h}", [P, 2, CT, KW, PAIRS, WPAD], F16) for h in range(2)]
    NU = 4
    Uf = [sb(ctx, f"Uf{i}", [P, PAIRS, WPAD]) for i in range(NU)]
    dwt = [sb(ctx, f"dwt{t}", [P, CT, TROWS * PITCH]) for t in range(2)]
    s1 = [sb(ctx, f"s1{c}", [P, TPAIRS, W]) for c in range(CT)]
    yraw = [sb(ctx, f"yraw{c}", [P, TPAIRS, 2, W]) for c in range(CT)]
    rep = [sb(ctx, f"rep{c}", [P, TROWS, W]) for c in range(CT)]
    fin = [sb(ctx, f"fin{c}", [P, TROWS, W]) for c in range(CT)]

    xb_loaded = [sem(f"xb_loaded{i}") for i in range(2)]
    pad_zero = sem("dense_padding_zeroed")
    xn_ready = sem("xn_ready")
    uf_ready = [sem(f"uf_ready{i}") for i in range(NU)]
    u_high = [sem(f"u_high{i}") for i in range(NU)]
    u_low = [sem(f"u_low{i}") for i in range(NU)]
    m_full = [[sem(f"m_full{c}{k}") for k in range(KW)] for c in range(CT)]
    s1_ready = [sem(f"s1_ready{c}") for c in range(CT)]
    even_ready = [sem(f"even_half{c}") for c in range(CT)]
    y_ready = [sem(f"y_ready{c}") for c in range(CT)]
    rep_ready = [sem(f"rep_ready{c}") for c in range(CT)]
    z_ready = [sem(f"z_ready{c}") for c in range(CT)]
    fin_ready = [sem(f"fin_ready{c}") for c in range(CT)]
    sum_ready = [sem(f"sum_ready{c}") for c in range(CT)]
    out_stored = [sem(f"out_stored{c}") for c in range(CT)]
    dw_loaded = [sem(f"dw_tile_loaded{t}") for t in range(2)]

    ORDER = (1, 2, 0, 3)
    GROUPS = [(t, c) for t in range(2) for c in range(CT)]
    PIECES = [(ci, k) for ci in range(CT) for k in range(KW)]

    def images(eng, image, parity):
        if parity:
            with eng.Fori(0, B // 2 - 1) as i:
                image(i * 2, i, 0, True)
                image(i * 2 + 1, i, 1, True)
            image(B - 2, B // 2 - 1, 0, True)
            image(B - 1, B // 2 - 1, 1, False)
        else:
            with eng.Fori(0, B - 1) as b:
                image(b, None, None, True)
            image(B - 1, None, None, False)

    block = ctx.enter_context(nc.Block())

    @block.sync
    def _(sp):
        def load_x(b, i, par):
            if not (isinstance(b, int) and b == 0):
                done = (b - 1) * (2 * CT)
                sp.wait_ge(xn_ready, done)
                for c in range(CT):
                    sp.wait_ge(sum_ready[c], done)
            for ci in range(CT):
                src = x3[bass.ds(b, 1), ci * P:(ci + 1) * P, :].rearrange("a c q -> c (a q)")
                sp.dma_start(Xb[par][:, ci].rearrange("p y x -> p (y x)"), src).then_inc(xb_loaded[par], 16)

        load_x(0, 0, 0)

        def image(b, i, par, more):
            for h in range(2):
                if h == 0 and more:
                    load_x(b + 1, i + par, 1 - par)
                for t in range(2):
                    load_dw_at(b, h, t)
                for t, c in GROUPS:
                    sp.wait_ge(sum_ready[c], b * 4 + h * 2 + t + 1)
                    dst = out3[bass.ds(b, 1), c * P:(c + 1) * P,
                               (h * STEP_ROWS + t * TROWS) * W:(h * STEP_ROWS + (t + 1) * TROWS) * W]
                    sp.dma_start(dst.rearrange("a c q -> c (a q)"), fin[c][:].rearrange("p y x -> p (y x)")
                                 ).then_inc(out_stored[c], 16)

        def load_dw_at(b, h, t):
            for c in range(CT):
                sp.wait_ge(z_ready[c], b * 4 + h * 2)
            q = (h * STEP_ROWS + t * TROWS) * PITCH
            src = dw_d[bass.ds(b, 1), :, q:q + TROWS * PITCH].rearrange("a (k p) q -> p k (a q)", p=P)
            sp.dma_start(dwt[t][:], src).then_inc(dw_loaded[t], 16)

        images(sp, image, True)
        for c in range(CT):
            sp.wait_ge(out_stored[c], 16 * 4 * B)

    @block.tensor
    def _(pe):
        def image(b, i, par, more):
            for h in range(2):
                for n in range(NU):
                    pe.wait_ge(u_low[n], (b * 2 + h + 1) * (len(PIECES) // NU))
                for t, c in GROUPS:
                    for k in ORDER:
                        acc = bank[c * KW + k]
                        pe.wait_ge(y_ready[c] if k in (0, 3) else even_ready[c],
                                   (b * 4 + h * 2 + t) * (1 if k in (0, 3) else 2))
                        n = 0
                        for ci in range(CT):
                            for dx in range(3):
                                for zw, zx in ((0, 0), (0, 1), (1, 0)):
                                    last = nc.tensor.matmul(
                                        acc[:, 0:N3], wt[:, ci, k, dx, zw, c * P:(c + 1) * P],
                                        U[h][:, zx, ci, k, t * TPAIRS:(t + 1) * TPAIRS, dx:dx + W],
                                        start=(n == 0), stop=(n == 6 * CT + 3 * CT - 1))
                                    n += 1
                        last.then_inc(m_full[c][k], 1)
        images(pe, image, False)

    @block.scalar
    def _(act):
        def take_high(kk, h, n):
            act.wait_ge(uf_ready[n % NU], kk * (len(PIECES) // NU) + n // NU + 1)
            ci, k = PIECES[n]
            nc.scalar.copy(U[h][:, 0, ci, k], Uf[n % NU][:]).then_inc(u_high[n % NU], 1)

        for n in range(len(PIECES)):
            take_high(0, 0, n)

        def image(b, i, par, more):
            for h in range(2):
                act.wait_ge(m_full[CT - 1][ORDER[-1]], b * 4 + h * 2)
                for g, (t, c) in enumerate(GROUPS):
                    tile = b * 4 + h * 2 + t
                    if more or h == 0:
                        for n in (2 * g, 2 * g + 1):
                            take_high(b * 2 + h + 1, 1 - h, n)
                    act.wait_ge(m_full[c][1], tile + 1)
                    nc.scalar.copy(s1[c][:].rearrange("p y x -> p (y x)"), bank[c * KW + 1][:, 0:N3]
                                   ).then_inc(s1_ready[c], 1)
                    act.wait_ge(y_ready[c], tile + 1)
                    nc.scalar.activation(rep[c][:].rearrange("p y x -> p (y x)"),
                                         yraw[c][:].rearrange("p y r x -> p (y r x)"), ACT.Silu,
                                         bias=bias1[:, c:c + 1], scale=scale1[:, c:c + 1]).then_inc(rep_ready[c], 1)
                    act.wait_ge(z_ready[c], tile + 1)
                    act.wait_ge(out_stored[c], tile * 16)
                    nc.scalar.activation(fin[c][:].rearrange("p y x -> p (y x)"),
                                         rep[c][:].rearrange("p y x -> p (y x)"), ACT.Silu,
                                         bias=bias3[:, c:c + 1], scale=fold3[:, c:c + 1]).then_inc(fin_ready[c], 1)
        images(act, image, False)

    @block.gpsimd
    def _(pool):
        def image(b, i, par, more):
            for h in range(2):
                for t, c in GROUPS:
                    pool.wait_ge(fin_ready[c], b * 4 + h * 2 + t + 1)
                    r = h * STEP_ROWS + t * TROWS
                    nc.gpsimd.tensor_tensor(fin[c][:], fin[c][:], Xb[par][:, c, r:r + TROWS, :], ALU.add
                                            ).then_inc(sum_ready[c], 1)
        images(pool, image, True)

    @block.vector
    def _(dve):
        def normalise(b, i, par, h, kk):
            if h == 0:
                dve.wait_ge(xb_loaded[par], (i + 1) * 16 * CT)
            lo = 0 if h == 0 else STEP_ROWS - 1
            for n in range(NU):
                dve.wait_ge(uf_ready[n], kk * (len(PIECES) // NU))
            for ci in range(CT):
                mean = stats[:, ci, bass.ds(b, 1), 0]
                rstd = stats[:, ci, bass.ds(b, 1), 1]
                last = nc.vector.tensor_scalar(xn[:, ci, 1:STEP_ROWS + 2, 1:W + 1],
                                               Xb[par][:, ci, lo:lo + STEP_ROWS + 1, :], mean, rstd,
                                               ALU.subtract, ALU.mult)
                last.then_inc(xn_ready, 1)
            dve.wait_ge(xn_ready, (kk + 1) * CT)

        def transform(kk, h, n):
            ci, k = PIECES[n]
            a, b_, op = ((0, 2, ALU.subtract), (1, 2, ALU.add), (2, 1, ALU.subtract), (1, 3, ALU.subtract))[k]
            dve.wait_ge(u_low[n % NU], kk * (len(PIECES) // NU) + n // NU)
            rows = [xn[:, ci, h + j:h + j + 2 * PAIRS - 1:2, :] for j in (a, b_)]
            nc.vector.tensor_tensor(Uf[n % NU][:], rows[0], rows[1], op).then_inc(uf_ready[n % NU], 1)

        def take_low(kk, h, n):
            ci, k = PIECES[n]
            dve.wait_ge(u_high[n % NU], kk * (len(PIECES) // NU) + n // NU + 1)
            nc.vector.tensor_tensor(U[h][:, 1, ci, k], Uf[n % NU][:], U[h][:, 0, ci, k], ALU.subtract
                                    ).then_inc(u_low[n % NU], 1)

        nc.vector.memset(xn[:], 0.0).then_inc(pad_zero, 1)
        dve.wait_ge(pad_zero, 1)
        normalise(0, 0, 0, 0, 0)
        for n in range(0, len(PIECES), 2):
            transform(0, 0, n)
            transform(0, 0, n + 1)
            take_low(0, 0, n)
            take_low(0, 0, n + 1)

        def image(b, i, par, more):
            for h in range(2):
                kk = b * 2 + h + 1
                prepare = more or h == 0
                if prepare:
                    if h == 0:
                        normalise(b, i, par, 1, kk)
                    else:
                        normalise(b + 1, i + par, 1 - par, 0, kk)
                for g, (t, c) in enumerate(GROUPS):
                    tile = b * 4 + h * 2 + t
                    even, odd = yraw[c][:, :, 0, :], yraw[c][:, :, 1, :]

                    def product(k):
                        return bank[c * KW + k][:, 0:N3].rearrange("p (y x) -> p y x", x=W)

                    if prepare:
                        transform(kk, 1 - h, 2 * g)
                        transform(kk, 1 - h, 2 * g + 1)
                    dve.wait_ge(s1_ready[c], tile + 1)
                    dve.wait_ge(m_full[c][2], tile + 1)
                    nc.vector.tensor_tensor(even, s1[c][:], product(2), ALU.add).then_inc(even_ready[c], 1)
                    nc.vector.tensor_tensor(odd, s1[c][:], product(2), ALU.subtract).then_inc(even_ready[c], 1)
                    if prepare:
                        take_low(kk, 1 - h, 2 * g)
                        take_low(kk, 1 - h, 2 * g + 1)
                    dve.wait_ge(even_ready[c], (tile + 1) * 2)
                    dve.wait_ge(m_full[c][0], tile + 1)
                    nc.vector.tensor_tensor(even, even, product(0), ALU.add)
                    dve.wait_ge(m_full[c][3], tile + 1)
                    nc.vector.tensor_tensor(odd, odd, product(3), ALU.subtract).then_inc(y_ready[c], 1)
                    dve.wait_ge(rep_ready[c], tile + 1)
                    dve.wait_ge(dw_loaded[t], (b * 2 + h + 1) * 16)
                    dwv = dwt[t][:, c, :].rearrange("p (y x) -> p y x", x=PITCH)[:, :, 0:W]
                    nc.vector.scalar_tensor_tensor(rep[c][:], dwv, dw_scale[:, c:c + 1], rep[c][:],
                                                   ALU.mult, ALU.add).then_inc(z_ready[c], 1)
        images(dve, image, True)


_NAMES = ["x"] + ["L0_conv_" + n for n in ("w3", "g1", "b1", "m1", "v1", "w1", "g2", "b2", "m2", "v2",
                                           "dw7", "dwk", "g3", "b3", "m3", "v3")]


def kernel(**inputs):
    import numpy as _np
    import concourse.bacc as _bacc
    from concourse import mybir as _mybir
    from concourse.bass_utils import run_bass_kernel_spmd as _run

    nc = _bacc.Bacc("TRN2", target_bir_lowering=False, num_devices=1)
    arrays, args = {}, []
    p = _np.arange(P)
    consts = {
        "ident": _np.eye(P, dtype=_np.float32),
        "gmat": ((p[:, None] // (GROUP_C * BH) == p[None, :] // (GROUP_C * BH))
                 & (p[:, None] % BH == p[None, :] % BH)).astype(_np.float32) / _np.float32(GROUP_C),
    }
    for name in _NAMES + list(consts):
        a = _np.ascontiguousarray(inputs[name] if name in inputs else consts[name])
        arrays[f"in_{name}"] = a
        args.append(nc.dram_tensor(f"in_{name}", a.shape, _mybir.dt.from_np(a.dtype), kind="ExternalInput").ap())
    args.append(nc.dram_tensor("out_0", (B, C, H, W), F32, kind="ExternalOutput").ap())
    build(nc, *args)
    r = _run(nc, [arrays], core_ids=[0])
    return r.results[0]["out_0"]
```

```python
from contextlib import ExitStack

import numpy as np
import concourse.bass as bass
from concourse import mybir

F32 = mybir.dt.float32
F16 = mybir.dt.float16
ALU = mybir.AluOpType
ACT = mybir.ActivationFunctionType
AXX = mybir.AxisListType.X

P = 128
B, C, H, W = 16, 256, 56, 56
HW = H * W
CT = C // P
GROUP_C = C // 32
GN_EPS = 1e-5
BN_EPS = 1e-5
XS = 32.0
WS = 256.0

K7 = 7
R7 = K7 // 2
PITCH = W + R7
REACH = R7 * PITCH + R7
OUT_BLOCKS = -(-(PITCH * (H - 1) + W) // P)
TAP_BLOCKS = 4
LEAD = REACH - P
IN_BLOCKS = OUT_BLOCKS + 1
STRIP = TAP_BLOCKS * P
VEC = STRIP + P
CC = 16
CHUNKS = C // CC
BH = B // 2
SG = 4
SGROUPS = CC // SG
IN_BATCHES = -(-IN_BLOCKS // 4)
HALF_BLOCKS = OUT_BLOCKS // 2

KW = 6
WPAD = W + 2
STEP_ROWS = H // 2
X_ROWS = STEP_ROWS + 1
QUADS = STEP_ROWS // 4
N3 = QUADS * W
NT = STEP_ROWS * W


def strip_centre():
    return P + LEAD + P - 1


def build(nc, x, w3, g1, b1, m1, v1, w1, g2, b2, m2, v2, dw7, dwk, g3, b3, m3, v3, ident_d, gmat_d, out):
    root = ExitStack()

    def sb(ctx, name, shape, dt=F32):
        return ctx.enter_context(nc.sbuf_tensor(name, shape, dt))

    def sem(name):
        return root.enter_context(nc.semaphore(name))

    x3 = x.rearrange("b c h w -> b c (h w)")
    out3 = out.rearrange("b c h w -> b c (h w)")
    vec_d = nc.dram_tensor("strip_vectors", [C, 2, VEC], F16, kind="Internal").ap()
    dw_d = nc.dram_tensor("depthwise_out", [B, C, OUT_BLOCKS * P], F32, kind="Internal").ap()
    st_d = nc.dram_tensor("gn_stats", [B, C, 2], F32, kind="Internal").ap()

    with root:
        bank = [root.enter_context(nc.psum_tensor(f"bank{i}", [P, 512], F32)) for i in range(8)]
        ident = sb(root, "ident", [P, P])
        dw_scale = sb(root, "dw_scale", [P, CT])
        depthwise(nc, sb, sem, bank, ident, ident_d, dw_scale, dw7, dwk, x3, vec_d, dw_d, st_d, gmat_d)
        dense(nc, sb, sem, bank, ident, dw_scale, w3, w1, (g1, b1, m1, v1), (g2, b2, m2, v2),
              (g3, b3, m3, v3), x3, dw_d, st_d, out3)
    return nc


def wait(eng, sem, value):
    if not isinstance(value, int) or value > 0:
        eng.wait_ge(sem, value)


def depthwise(nc, sb, sem, bank, ident, ident_d, dw_scale, dw7, dwk, x3, vec_d, dw_d, st_d, gmat_d):
    T, CV, BK, GS = bank[0:2], bank[2:6], bank[6], bank[7]
    with ExitStack() as ctx:
        gmat = sb(ctx, "gmat", [P, P])
        Xa = [sb(ctx, f"Xa{h}", [P, HW]) for h in range(2)]
        Xp = [sb(ctx, f"Xp{h}", [P, IN_BLOCKS * P]) for h in range(2)]
        D = [sb(ctx, f"D{s}", [P, 2, CC, IN_BLOCKS * B], F16) for s in range(2)]
        S = [sb(ctx, f"S{g}", [P, SG, 2, STRIP], F16) for g in range(SGROUPS)]
        with ExitStack() as early:
            dwa = sb(early, "dwa", [P, CT, K7 * K7])
            dwb = sb(early, "dwb", [P, CT, K7 * K7])
            dmax = sb(early, "dmax", [P, CT])
            dmin = sb(early, "dmin", [P, CT])
            dinv = sb(early, "dinv", [P, CT])
            vec = sb(early, "vec", [P, CT, VEC])
            vech = sb(early, "vech", [P, CT, 2, VEC], F16)
        Y = [sb(ctx, f"Y{s}", [P, 2, OUT_BLOCKS, CC * BH]) for s in range(2)]
        O = [sb(ctx, f"O{q}", [P, HALF_BLOCKS * P]) for q in range(2)]
        bn = [sb(ctx, f"bn{h}", [P, 7, 6]) for h in range(2)]
        mv = [sb(ctx, f"mv{h}", [P, 2]) for h in range(2)]
        dev = [sb(ctx, f"dev{h}", [P, 2]) for h in range(2)]
        var = [sb(ctx, f"var{h}", [P, 1]) for h in range(2)]
        std = [sb(ctx, f"std{h}", [P, 1]) for h in range(2)]
        neg = [sb(ctx, f"neg{h}", [P, 1]) for h in range(2)]
        root_ = [sb(ctx, f"rsqrt{h}", [P, 3]) for h in range(2)]
        st = [[sb(ctx, f"st{s}{h}", [P, 2]) for h in range(2)] for s in range(2)]

        s_const, s_zero = sem("constants_loaded"), sem("padding_zeroed")
        s_dw, s_filter, s_vec = sem("dw_loaded"), sem("filter_steps"), sem("vectors_stored")
        xa_loaded = [sem(f"xa_loaded{h}") for h in range(2)]
        xp_ready = [sem(f"xp_ready{h}") for h in range(2)]
        t_full = [sem(f"t_full{i}") for i in range(2)]
        t_high = [sem(f"t_high{i}") for i in range(2)]
        t_low = [sem(f"t_low{i}") for i in range(2)]
        s_loaded = [sem(f"s_loaded{g}") for g in range(SGROUPS)]
        cv_full = [sem(f"cv_full{i}") for i in range(4)]
        cv_free = [sem(f"cv_free{i}") for i in range(4)]
        bk_full, bk_free = sem("bk_full"), sem("bk_free")
        o_stored = [sem(f"o_stored{q}") for q in range(2)]
        st_stored = [sem(f"st_stored{s}") for s in range(2)]
        q_pieces = [sem(f"bn_pieces{h}") for h in range(2)]
        q_aggr = [sem(f"bn_aggr{h}") for h in range(2)]
        q_gmean = [sem(f"group_mean{h}") for h in range(2)]
        q_diff = [sem(f"mean_diff{h}") for h in range(2)]
        q_dev = [sem(f"deviation{h}") for h in range(2)]
        q_gvar = [sem(f"group_var{h}") for h in range(2)]
        q_var = [sem(f"group_var_scaled{h}") for h in range(2)]
        q_newton = [sem(f"rsqrt_steps{h}") for h in range(2)]
        q_std = [sem(f"group_std{h}") for h in range(2)]
        q_rstd = [sem(f"group_rstd{h}") for h in range(2)]

        def chunks(eng, step):
            for n in range(3):
                step(n, n // 2, n % 2)
            with eng.Fori(1, (CHUNKS - 4) // 2) as i:
                step(i * 2 + 1, i, 1)
                step(i * 2 + 2, i + 1, 0)
            for n in range(CHUNKS - 3, CHUNKS):
                step(n, n // 2, n % 2)

        def has(n, last):
            return not isinstance(n, int) or n <= last

        def in_blocks(k):
            return range(4 * k, min(4 * k + 4, IN_BLOCKS))

        IN_SLOTS = [(h, k) for h in range(2) for k in range(IN_BATCHES)]
        OUT_SLOTS = [(h, q, range(4 * k, min(4 * k + 4, HALF_BLOCKS))) for h in range(2) for q in range(2)
                     for k in range(4)]

        FILTER_STEPS = 11

        block = ctx.enter_context(nc.Block())

        @block.gpsimd
        def _(pool):
            def load_x(n, h):
                wait(pool, xp_ready[h], n)
                src = x3[h * BH:(h + 1) * BH, bass.ds(n * CC, CC), :].rearrange("b c q -> c b q")
                pool.dma_start(Xa[h][:], src).then_inc(xa_loaded[h], 16)

            for h in range(2):
                load_x(0, h)
            for h in range(2):
                nc.gpsimd.memset(Xp[h][:], 0.0).then_inc(s_zero, 1)
            with pool.Fori(1, CHUNKS) as n:
                for h in range(2):
                    load_x(n, h)

        @block.sync
        def _(sp):
            with nc.allow_non_contiguous_dma(reason="small"):
                sp.dma_start(dwa[:], dw7.rearrange("(k p) o y x -> p k (o y x)", p=P)).then_inc(s_dw, 16)
                sp.dma_start(dwb[:], dwk.rearrange("(k p) o y x -> p k (o y x)", p=P)).then_inc(s_dw, 16)
            sp.dma_start(gmat[:], gmat_d).then_inc(s_const, 16)
            sp.dma_start(ident[:], ident_d).then_inc(s_const, 16)
            sp.wait_ge(s_filter, FILTER_STEPS)
            for k in range(CT):
                sp.dma_start(vec_d[k * P:(k + 1) * P], vech[:, k]).then_inc(s_vec, 16)
            sp.wait_ge(s_vec, 16 * CT)

            def load_strips(n, g):
                v = vec_d[bass.ds(n * CC + g * SG, SG)]
                src = bass.AP(v.tensor, v.offset, [[1, P], [VEC, SG * 2], [1, STRIP]])
                sp.dma_start(S[g][:].rearrange("p c z m -> p (c z) m"), src).then_inc(s_loaded[g], 16)

            def store_stats(n, m, s):
                for h in range(2):
                    sp.wait_ge(q_rstd[h], n + 1)
                    dst = st_d[h * BH:(h + 1) * BH, bass.ds(n * CC, CC), :].rearrange("b c v -> c b v")
                    sp.dma_start(dst, st[s][h][:]).then_inc(st_stored[s], 16)

            def store_out(n, p):
                h, q = p // 2, p % 2
                sp.wait_ge(bk_free, n * 16 + 4 * p + 4)
                dst = dw_d[h * BH:(h + 1) * BH, bass.ds(n * CC, CC),
                           q * HALF_BLOCKS * P:(q + 1) * HALF_BLOCKS * P].rearrange("b c q -> c b q")
                sp.dma_start(dst, O[q][:]).then_inc(o_stored[q], 16)

            for g in range(SGROUPS):
                load_strips(0, g)
            store_stats(0, 0, 0)
            store_stats(1, 0, 1)

            def step(n, m, s):
                for g in range(SGROUPS):
                    if has(n, CHUNKS - 2):
                        sp.wait_ge(cv_full[SG - 1], n * SGROUPS + g + 1)
                        load_strips(n + 1, g)
                    if not (isinstance(n, int) and n == 0):
                        store_out(n - 1, g)
                if has(n, CHUNKS - 3):
                    store_stats(n + 2, m + 1, s)

            chunks(sp, step)
            for p in range(4):
                store_out(CHUNKS - 1, p)
            for q in range(2):
                sp.wait_ge(o_stored[q], 16 * 2 * CHUNKS)
            for s in range(2):
                sp.wait_ge(st_stored[s], 16 * CHUNKS)

        @block.tensor
        def _(pe):
            def group_mean(n, h):
                wait(pe, q_var[1 - h], n + h)
                pe.wait_ge(q_aggr[h], n + 1)
                nc.tensor.matmul(GS[:, 2 * h:2 * h + 1], gmat[:], mv[h][:, 0:1], start=True, stop=True
                                 ).then_inc(q_gmean[h], 1)

            def group_var(n, h):
                pe.wait_ge(q_dev[h], n + 1)
                nc.tensor.matmul(GS[:, 2 * h + 1:2 * h + 2], gmat[:], dev[h][:, 1:2], start=True, stop=True
                                 ).then_inc(q_gvar[h], 1)

            def transpose_in(n, slot):
                h, k = IN_SLOTS[slot]
                if k == 0:
                    pe.wait_ge(xp_ready[h], n + 1)
                wait(pe, t_low[slot % 2], n * 7 + slot // 2)
                for j, b in enumerate(in_blocks(k)):
                    last = nc.tensor.transpose(T[slot % 2][:, j * P:(j + 1) * P],
                                               Xp[h][:, b * P:(b + 1) * P], ident[:])
                last.then_inc(t_full[slot % 2], 1)

            def transpose_out(n, s, slot):
                h, q, blocks = OUT_SLOTS[slot]
                if slot == 0:
                    for i in range(4):
                        pe.wait_ge(cv_free[i], (n + 1) * 4)
                wait(pe, bk_free, n * 16 + slot)
                for j, b in enumerate(blocks):
                    last = nc.tensor.transpose(BK[:, j * P:(j + 1) * P],
                                               Y[s][:, h, q * HALF_BLOCKS + b, :], ident[:])
                last.then_inc(bk_full, 1)

            def convolve(n, s, c):
                if c == 0:
                    for i in range(2):
                        pe.wait_ge(t_low[i], (n + 1) * 7)
                if c % SG == 0:
                    pe.wait_ge(s_loaded[c // SG], (n + 1) * 16)
                wait(pe, cv_free[c % 4], n * 4 + c // 4)
                strip, data, acc = S[c // SG], D[s], CV[c % 4]
                n_out = OUT_BLOCKS * B
                for z, (hs, hd) in enumerate(((0, 0), (0, 1), (1, 0))):
                    for j in (1, 2, 0, 3):
                        lo = B if j == 0 else 0
                        hi = n_out - B if j == 3 else n_out
                        last = nc.tensor.matmul(
                            acc[:, lo:hi], strip[:, c % SG, hs, j * P:(j + 1) * P],
                            data[:, hd, c, lo + (j - 1) * B:hi + (j - 1) * B],
                            start=(z == 0 and j == 1), stop=(z == 2 and j == 3))
                last.then_inc(cv_full[c % 4], 1)

            pe.wait_ge(s_const, 32)
            for n in range(2):
                for h in range(2):
                    group_mean(n, h)
                    group_var(n, h)
                if n == 0:
                    for slot in range(len(IN_SLOTS)):
                        transpose_in(0, slot)

            def step(n, m, s):
                first = isinstance(n, int) and n == 0
                for c in range(CC):
                    convolve(n, s, c)
                    if not first:
                        transpose_out(n - 1, 1 - s, c)
                    if c < len(IN_SLOTS) and has(n, CHUNKS - 2):
                        transpose_in(n + 1, c)
                    if has(n, CHUNKS - 3):
                        if c in (5, 9):
                            group_mean(n + 2, c // 4 - 1)
                        if c in (7, 11):
                            group_var(n + 2, c // 4 - 1)

            chunks(pe, step)
            for slot in range(CC):
                transpose_out(CHUNKS - 1, 1, slot)

        @block.scalar
        def _(act):
            def take_high(n, s, slot):
                h, k = IN_SLOTS[slot]
                nb = len(in_blocks(k))
                act.wait_ge(t_full[slot % 2], n * 7 + slot // 2 + 1)
                dst = D[s][:, 0].rearrange("p c (k b) -> p k c b", b=B)[:, 4 * k:4 * k + nb, :, h * BH:(h + 1) * BH]
                src = T[slot % 2][:, 0:nb * P].rearrange("p (k c b) -> p k c b", c=CC, b=BH)
                nc.scalar.copy(dst, src).then_inc(t_high[slot % 2], 1)

            def take_conv(n, s, c):
                act.wait_ge(cv_full[c % 4], n * 4 + c // 4 + 1)
                dst = Y[s][:, :, :, c * BH:(c + 1) * BH].rearrange("p h k b -> p k h b")
                src = CV[c % 4][:, 0:OUT_BLOCKS * B].rearrange("p (k h b) -> p k h b", h=2, b=BH)
                nc.scalar.copy(dst, src).then_inc(cv_free[c % 4], 1)

            def take_out(n, slot):
                h, q, blocks = OUT_SLOTS[slot]
                if slot % 4 == 0:
                    wait(act, o_stored[q], (n * 2 + h) * 16)
                act.wait_ge(bk_full, n * 16 + slot + 1)
                dst = O[q][:, blocks[0] * P:(blocks[-1] + 1) * P].rearrange("p (k m) -> p k m", m=P)
                src = BK[:, 0:len(blocks) * P].rearrange("p (k m) -> p k m", m=P)
                nc.scalar.copy(dst, src[:, :, ::-1]).then_inc(bk_free, 1)

            def group_std(n, h):
                act.wait_ge(q_var[h], n + 1)
                nc.scalar.activation(std[h][:], var[h][:], ACT.Sqrt).then_inc(q_std[h], 1)

            act.wait_ge(s_vec, 16 * CT)
            for n in range(2):
                for h in range(2):
                    group_std(n, h)
                if n == 0:
                    for slot in range(len(IN_SLOTS)):
                        take_high(0, 0, slot)

            def step(n, m, s):
                first = isinstance(n, int) and n == 0
                for c in range(CC):
                    if c in (9, 13) and has(n, CHUNKS - 3):
                        group_std(n + 2, c // 4 - 2)
                    take_conv(n, s, c)
                    if not first:
                        take_out(n - 1, c)
                    if c < len(IN_SLOTS) and has(n, CHUNKS - 2):
                        take_high(n + 1, 1 - s, c)


            chunks(act, step)
            for slot in range(CC):
                take_out(CHUNKS - 1, slot)

        @block.vector
        def _(dve):
            def stat_piece(n, h, k):
                if k == 0:
                    dve.wait_ge(xa_loaded[h], (n + 1) * 16)
                nc.vector.bn_stats(bn[h][:, k, :], Xa[h][:, k * 448:(k + 1) * 448]).then_inc(q_pieces[h], 1)

            def stat_pieces_done(n, h):
                dve.wait_ge(q_pieces[h], (n + 1) * 7)

            def stat_aggregate(n, h):
                nc.vector.bn_aggr(mv[h][:], bn[h][:].rearrange("p k v -> p (k v)")).then_inc(q_aggr[h], 1)

            def stat_deviation(n, m, s, h):
                dve.wait_ge(q_gmean[h], n + 1)
                wait(dve, st_stored[s], m * 32)
                wait(dve, xp_ready[h], n)
                nc.vector.tensor_scalar(neg[h][:], GS[:, 2 * h:2 * h + 1], -1.0, None, ALU.mult)
                nc.vector.tensor_tensor(dev[h][:, 0:1], mv[h][:, 0:1], GS[:, 2 * h:2 * h + 1], ALU.subtract
                                        ).then_inc(q_diff[h], 1)
                dve.wait_ge(q_diff[h], n + 1)
                nc.vector.scalar_tensor_tensor(dev[h][:, 1:2], dev[h][:, 0:1], dev[h][:, 0:1], mv[h][:, 1:2],
                                               ALU.mult, ALU.add).then_inc(q_dev[h], 1)

            def stat_variance(n, h):
                dve.wait_ge(q_gvar[h], n + 1)
                nc.vector.tensor_scalar(var[h][:], GS[:, 2 * h + 1:2 * h + 2], GN_EPS, 1.0 / (XS * XS),
                                        ALU.add, ALU.mult).then_inc(q_var[h], 1)

            def normalise(n, s, h):
                r, t, u = (root_[h][:, i:i + 1] for i in range(3))
                dve.wait_ge(q_std[h], n + 1)
                nc.vector.reciprocal(r, std[h][:]).then_inc(q_newton[h], 1)
                dve.wait_ge(q_newton[h], n * 4 + 1)
                nc.vector.scalar_tensor_tensor(t, r, r, var[h][:], ALU.mult, ALU.mult).then_inc(q_newton[h], 1)
                dve.wait_ge(q_newton[h], n * 4 + 2)
                nc.vector.tensor_scalar(u, t, -0.5, 1.5, ALU.mult, ALU.add).then_inc(q_newton[h], 1)
                dve.wait_ge(q_newton[h], n * 4 + 3)
                nc.vector.tensor_tensor(st[s][h][:, 1:2], r, u, ALU.mult).then_inc(q_newton[h], 1)
                dve.wait_ge(q_newton[h], n * 4 + 4)
                nc.vector.tensor_tensor(st[s][h][:, 0:1], neg[h][:], st[s][h][:, 1:2], ALU.mult
                                        ).then_inc(q_rstd[h], 1)
                slot = IN_BATCHES * (h + 1) - 1
                if not (isinstance(n, int) and n == 0):
                    dve.wait_ge(t_full[slot % 2], n * 7 - 7 + slot // 2 + 1)
                dst = Xp[h][:, LEAD:LEAD + H * PITCH].rearrange("p (y x) -> p y x", x=PITCH)[:, :, 0:W]
                nc.vector.tensor_scalar(dst, Xa[h][:].rearrange("p (y x) -> p y x", x=W), neg[h][:],
                                        st[s][h][:, 1:2], ALU.add, ALU.mult).then_inc(xp_ready[h], 1)

            def take_low(n, s, slot):
                h, k = IN_SLOTS[slot]
                nb = len(in_blocks(k))
                dve.wait_ge(t_high[slot % 2], n * 7 + slot // 2 + 1)

                def part(z):
                    return D[s][:, z].rearrange("p c (k b) -> p k c b", b=B)[:, 4 * k:4 * k + nb, :, h * BH:(h + 1) * BH]

                src = T[slot % 2][:, 0:nb * P].rearrange("p (k c b) -> p k c b", c=CC, b=BH)
                nc.vector.tensor_tensor(part(1), src, part(0), ALU.subtract).then_inc(t_low[slot % 2], 1)

            def prepare_filters():
                done = 0

                def link(ins, n=1):
                    nonlocal done
                    ins.then_inc(s_filter, 1)
                    done += 1
                    if n:
                        dve.wait_ge(s_filter, done)

                link(nc.vector.memset(vec[:], 0.0), 0)
                dve.wait_ge(s_dw, 32)
                link(nc.vector.tensor_tensor(dwa[:], dwa[:], dwb[:], ALU.add))
                link(nc.vector.tensor_reduce(dmax[:], dwa[:], AXX, ALU.max), 0)
                link(nc.vector.tensor_reduce(dmin[:], dwa[:], AXX, ALU.min))
                link(nc.vector.scalar_tensor_tensor(dmax[:], dmin[:], -1.0, dmax[:], ALU.mult, ALU.max))
                link(nc.vector.tensor_scalar(dmax[:], dmax[:], 1e-30, None, ALU.max))
                nc.vector.tensor_scalar(dw_scale[:], dmax[:], 1.0 / (WS * XS), None, ALU.mult)
                link(nc.vector.reciprocal(dinv[:], dmax[:]))
                at = strip_centre() - REACH
                for k in range(CT):
                    rows = vec[:, k, at:at + K7 * PITCH].rearrange("p (y x) -> p y x", x=PITCH)[:, :, 0:K7]
                    link(nc.vector.tensor_scalar(rows, dwa[:, k, :].rearrange("p (y x) -> p y x", x=K7),
                                                 dinv[:, k:k + 1], WS, ALU.mult, ALU.mult), k == CT - 1)
                link(nc.vector.tensor_copy(vech[:, :, 0, :], vec[:]))
                link(nc.vector.tensor_tensor(vech[:, :, 1, :], vec[:], vech[:, :, 0, :], ALU.subtract), 0)
                assert done == FILTER_STEPS

            prepare_filters()
            dve.wait_ge(s_zero, 2)
            for n in range(2):
                for h in range(2):
                    for k in range(7):
                        stat_piece(n, h, k)
                    stat_pieces_done(n, h)
                    stat_aggregate(n, h)
                    stat_deviation(n, 0, n, h)
                    stat_variance(n, h)
                    if n == 0:
                        normalise(n, n, h)
                if n == 0:
                    for slot in range(len(IN_SLOTS)):
                        take_low(0, 0, slot)
            for h in range(2):
                normalise(1, 1, h)

            def step(n, m, s):
                for c in range(CC):
                    if c in (4, 8) and has(n, CHUNKS - 3):
                        stat_pieces_done(n + 2, c // 4 - 1)
                    if c < len(IN_SLOTS) and has(n, CHUNKS - 2):
                        take_low(n + 1, 1 - s, c)
                    if has(n, CHUNKS - 3):
                        for h in range(2):
                            k = c - 4 * h
                            if 0 <= k < 4:
                                for piece in range(2 * k, min(2 * k + 2, 7)):
                                    stat_piece(n + 2, h, piece)
                            if k == 4:
                                stat_aggregate(n + 2, h)
                            if k == 8:
                                stat_variance(n + 2, h)
                            if k == 6:
                                stat_deviation(n + 2, m + 1, s, h)
                        if c in (10, 14):
                            normalise(n + 2, s, c // 14)

            chunks(dve, step)


def dense(nc, sb, sem, bank, ident, dw_scale, w3, w1, bn1, bn2, bn3, x3, dw_d, st_d, out3):
    ctx = ExitStack()
    with ctx:
        wt = sb(ctx, "wt", [P, CT, KW, 3, 2, C], F16)
        scale1 = sb(ctx, "scale1", [P, CT])
        bias1 = sb(ctx, "bias1", [P, CT])
        fold3 = sb(ctx, "fold3", [P, CT])
        bias3 = sb(ctx, "bias3", [P, CT])
        X = [sb(ctx, f"X{h}", [P, CT, X_ROWS, W]) for h in range(2)]
        xn = [sb(ctx, f"xn{c}", [P, STEP_ROWS + 3, WPAD]) for c in range(CT)]
        U = [sb(ctx, f"U{h}", [P, 2, CT, KW, QUADS, WPAD], F16) for h in range(2)]
        Uf = [sb(ctx, f"Uf{c}", [P, KW, QUADS, WPAD]) for c in range(CT)]
        stp = [sb(ctx, f"stp{h}", [P, CT, 2]) for h in range(2)]
        tmp = [sb(ctx, f"tmp{i}", [P, QUADS, WPAD]) for i in range(4)]
        with ExitStack() as early:
            wn = sb(early, "wn", [P, CT, C, 9])
            wc = sb(early, "wc", [P, CT, C])
            wk = sb(early, "wk", [P, CT, KW, 3, C])
            ws = sb(early, "ws", [P, 3, C])
            wh = sb(early, "wh", [P, 3, C])
            pn = sb(early, "pn", [P, 3, 4, CT])
            sd = sb(early, "sd", [P, 3, CT])
            rs = sb(early, "rs", [P, 3, CT])
            rt = sb(early, "rt", [P, 3, CT])
            fold = sb(early, "fold", [P, 3, CT])
            wmax = sb(early, "wmax", [P, CT])
            wmin = sb(early, "wmin", [P, CT])
            winv = sb(early, "winv", [P, CT])
        dwt = [sb(ctx, f"dwt{c}", [P, STEP_ROWS * PITCH]) for c in range(CT)]
        xr = [sb(ctx, f"xr{c}", [P, NT]) for c in range(CT)]
        y = [sb(ctx, f"y{c}", [P, QUADS, 4, W]) for c in range(CT)]
        rep = [sb(ctx, f"rep{c}", [P, NT]) for c in range(CT)]
        first = [[sb(ctx, f"first{c}{i}", [P, QUADS, W]) for i in range(2)] for c in range(CT)]
        sums = [sb(ctx, f"sum{i}", [P, QUADS, W]) for i in range(2)]
        diffs = [sb(ctx, f"diff{i}", [P, QUADS, W]) for i in range(2)]

        w_loaded, bn_loaded = sem("w_loaded"), sem("bn_loaded")
        w_step, bn_sqrt = sem("weight_steps"), sem("bn_sqrt")
        wt_full = [sem(f"wt_full{i}") for i in range(2)]
        wt_high = [sem(f"wt_high{i}") for i in range(2)]
        wt_low = [sem(f"wt_low{i}") for i in range(2)]
        pad_zero = sem("dense_padding_zeroed")
        x_loaded = [sem(f"x_loaded{h}") for h in range(2)]
        xn_ready = [sem(f"xn_ready{c}") for c in range(CT)]
        t_ready = sem("transform_sums")
        u_ready = [sem(f"u_ready{c}") for c in range(CT)]
        u_high = [sem(f"u_high{c}") for c in range(CT)]
        u_low = [sem(f"u_low{c}") for c in range(CT)]
        full = [sem(f"product_full{k}") for k in range(KW)]
        free = [sem(f"product_free{k}") for k in range(KW - 1)]
        y_part = [sem(f"y_part{c}") for c in range(CT)]
        y_ready = [sem(f"y_ready{c}") for c in range(CT)]
        rep_ready = [sem(f"rep_ready{c}") for c in range(CT)]
        z_ready = [sem(f"z_ready{c}") for c in range(CT)]
        f_ready = [sem(f"f_ready{c}") for c in range(CT)]
        sum_ready = [sem(f"sum_ready{c}") for c in range(CT)]
        out_stored = [sem(f"out_stored{c}") for c in range(CT)]
        dwt_loaded = [sem(f"dwt_loaded{c}") for c in range(CT)]
        xr_loaded = [sem(f"xr_loaded{c}") for c in range(CT)]

        ORDER = (1, 2, 3, 4, 0, 5)
        BATCHES = [(co, ci, k) for co in range(CT) for k in range(KW) for ci in range(CT)]
        HALVES = 2
        PER = KW // HALVES
        WEIGHT_STEPS = [33, 50]
        T_STEPS = 6

        def slot_bank(g, i):
            return bank[(g * KW + i) % 8]

        def images(eng, image):
            image(0, True)
            with eng.Fori(1, B - 1) as b:
                image(b, True)
            image(B - 1, False)

        def previous(b, h, c):
            if c == 1:
                return b * 2 + h, h, b, 0
            if isinstance(b, int) and b == 0 and h == 0:
                return None
            return b * 2 + h - 1, 1 - h, (b if h else b - 1), 1

        block = ctx.enter_context(nc.Block())

        @block.sync
        def _(sp):
            def load_x(b, h):
                r = 0 if h == 0 else STEP_ROWS - 1
                src = x3[bass.ds(b, 1), :, r * W:(r + X_ROWS) * W].rearrange("a (k p) q -> p k (a q)", p=P)
                sp.dma_start(X[h][:].rearrange("p k y x -> p k (y x)"), src).then_inc(x_loaded[h], 16)
                src = st_d[bass.ds(b, 1)].rearrange("a (k p) v -> p k (a v)", p=P)
                sp.dma_start(stp[h][:], src).then_inc(x_loaded[h], 16)

            def load_tile(b, h, c):
                k = b * 2 + h
                if isinstance(b, int) and b == 0 and h == 0:
                    for i in range(2):
                        sp.wait_ge(wt_full[i], len(BATCHES) // 2)
                wait(sp, z_ready[c], k)
                src = dw_d[bass.ds(b, 1), c * P:(c + 1) * P, h * STEP_ROWS * PITCH:(h + 1) * STEP_ROWS * PITCH]
                sp.dma_start(dwt[c][:], src.rearrange("a p q -> p (a q)")).then_inc(dwt_loaded[c], 16)
                wait(sp, sum_ready[c], k)
                src = x3[bass.ds(b, 1), c * P:(c + 1) * P, h * NT:(h + 1) * NT]
                sp.dma_start(xr[c][:], src.rearrange("a p q -> p (a q)")).then_inc(xr_loaded[c], 16)

            def store(k, h, b, c):
                sp.wait_ge(sum_ready[c], k + 1)
                dst = out3[bass.ds(b, 1), c * P:(c + 1) * P, h * NT:(h + 1) * NT]
                sp.dma_start(dst.rearrange("a p q -> p (a q)"), rep[c][:]).then_inc(out_stored[c], 16)

            load_x(0, 0)
            with nc.allow_non_contiguous_dma(reason="one value per channel"):
                for i, bns in enumerate((bn1, bn2, bn3)):
                    for j, a in enumerate(bns):
                        sp.dma_start(pn[:, i, j, :], a.rearrange("(k p) -> p k", p=P)).then_inc(bn_loaded, 16)
            sp.dma_start(wn[:].rearrange("p k i t -> p k (i t)"),
                         w3.rearrange("(k p) i y x -> p k (i y x)", p=P)).then_inc(w_loaded, 16)
            sp.dma_start(wc[:], w1.rearrange("(k p) i y x -> p k (i y x)", p=P)).then_inc(w_loaded, 16)
            load_x(0, 1)

            def image(b, more):
                for h in range(2):
                    if more:
                        for c in range(CT):
                            sp.wait_ge(xn_ready[c], b * 2 + h + 1)
                        load_x(b + 1, h)
                    for c in range(CT):
                        load_tile(b, h, c)
                        if before := previous(b, h, c):
                            store(*before)
            images(sp, image)
            store(2 * B - 1, 1, B - 1, 1)
            for c in range(CT):
                sp.wait_ge(out_stored[c], 16 * 2 * B)

        @block.gpsimd
        def _(pool):
            def add_residual(k, h, b, c):
                pool.wait_ge(f_ready[c], k + 1)
                pool.wait_ge(xr_loaded[c], k * 16 + 16)
                nc.gpsimd.tensor_tensor(rep[c][:], rep[c][:], xr[c][:], ALU.add).then_inc(sum_ready[c], 1)

            for c in range(CT):
                nc.gpsimd.memset(xn[c][:], 0.0).then_inc(pad_zero, 1)

            def image(b, more):
                for h in range(2):
                    for c in range(CT):
                        if before := previous(b, h, c):
                            add_residual(*before)
            images(pool, image)
            add_residual(2 * B - 1, 1, B - 1, 1)

        @block.tensor
        def _(pe):
            for n, (co, ci, k) in enumerate(BATCHES):
                pe.wait_ge(w_step, WEIGHT_STEPS[co])
                wait(pe, wt_low[n % 2], n // 2)
                for d in range(3):
                    last = nc.tensor.transpose(bank[n % 2][:, d * P:(d + 1) * P],
                                               wk[:, co, k, d, ci * P:(ci + 1) * P], ident[:])
                last.then_inc(wt_full[n % 2], 1)
            for i in range(2):
                pe.wait_ge(wt_low[i], len(BATCHES) // 2)

            def image(b, more):
                for h in range(2):
                    for c in range(CT):
                        pe.wait_ge(u_low[c], (b * 2 + h + 1) * HALVES)
                    for c in range(CT):
                        g = h * CT + c
                        for i, k in enumerate(ORDER):
                            j, back = (i - 2, 1) if i >= 2 else (i + 4, 2)
                            if j == KW - 1:
                                wait(pe, y_ready[(g - back) % CT], b * 2 + (g - back) // CT + 1)
                            else:
                                wait(pe, free[ORDER[j]], b * 4 + g - back + 1)
                            acc = slot_bank(g, i)[:, 0:N3]
                            n = 0
                            for ci in range(CT):
                                for dx in range(3):
                                    for zw, zx in ((0, 0), (0, 1), (1, 0)):
                                        last = nc.tensor.matmul(
                                            acc, wt[:, ci, k, dx, zw, c * P:(c + 1) * P],
                                            U[h][:, zx, ci, k, :, dx:dx + W],
                                            start=(n == 0), stop=(n == 9 * CT - 1))
                                        n += 1
                            last.then_inc(full[k], 1)
            images(pe, image)

        @block.scalar
        def _(act):
            def normalise(b, h, c):
                if c == 0:
                    act.wait_ge(x_loaded[h], b * 32 + 32)
                wait(act, u_ready[c], (b * 2 + h) * HALVES)
                nc.scalar.activation(xn[c][:, 1:X_ROWS + 1, 1:W + 1], X[h][:, c], ACT.Identity,
                                     bias=stp[h][:, c, 0:1], scale=stp[h][:, c, 1:2]).then_inc(xn_ready[c], 1)

            def take_high(k, h, c, half):
                act.wait_ge(u_ready[c], k * HALVES + half + 1)
                wait(act, full[ORDER[-1]], k * CT - CT)
                ks = slice(half * PER, (half + 1) * PER)
                nc.scalar.copy(U[h][:, 0, c, ks].rearrange("p k y x -> p (k y x)"),
                               Uf[c][:, ks].rearrange("p k y x -> p (k y x)")).then_inc(u_high[c], 1)

            def take_product(b, h, c, i):
                k = ORDER[i]
                act.wait_ge(full[k], b * 4 + h * CT + c + 1)
                wait(act, y_ready[c], b * 2 + h)
                nc.scalar.copy(first[c][i // 2][:].rearrange("p y x -> p (y x)"),
                               slot_bank(h * CT + c, i)[:, 0:N3]).then_inc(free[k], 1)

            def activate_first(k, h, b, c):
                act.wait_ge(y_ready[c], k + 1)
                wait(act, out_stored[c], k * 16)
                nc.scalar.activation(rep[c][:], y[c][:].rearrange("p q r x -> p (q r x)"), ACT.Silu,
                                     bias=bias1[:, c:c + 1], scale=scale1[:, c:c + 1]).then_inc(rep_ready[c], 1)

            def activate_last(k, h, b, c):
                act.wait_ge(z_ready[c], k + 1)
                nc.scalar.activation(rep[c][:], rep[c][:], ACT.Silu, bias=bias3[:, c:c + 1],
                                     scale=fold3[:, c:c + 1]).then_inc(f_ready[c], 1)

            act.wait_ge(pad_zero, CT)
            for c in range(CT):
                normalise(0, 0, c)
            for c in range(CT):
                for half in range(HALVES):
                    take_high(0, 0, c, half)
            for c in range(CT):
                normalise(0, 1, c)
            act.wait_ge(w_step, 1)
            nc.scalar.activation(sd[:], pn[:, :, 3, :], ACT.Sqrt).then_inc(bn_sqrt, 1)
            for n, (co, ci, k) in enumerate(BATCHES):
                act.wait_ge(wt_full[n % 2], n // 2 + 1)
                nc.scalar.copy(wt[:, ci, k, :, 0, co * P:(co + 1) * P],
                               bank[n % 2][:, 0:3 * P].rearrange("p (d m) -> p d m", m=P)).then_inc(wt_high[n % 2], 1)

            def image(b, more):
                for h in range(2):
                    for c in range(CT):
                        before = previous(b, h, c)
                        if before:
                            activate_first(*before)
                        take_product(b, h, c, 0)
                        if more or h == 0:
                            take_high(b * 2 + h + 1, 1 - h, c, 0)
                        if before:
                            activate_last(*before)
                        take_product(b, h, c, 2)
                        if more or h == 0:
                            take_high(b * 2 + h + 1, 1 - h, c, 1)
                        if more:
                            normalise(b + 1, h, c)
            images(act, image)
            activate_first(2 * B - 1, 1, B - 1, 1)
            activate_last(2 * B - 1, 1, B - 1, 1)

        @block.vector
        def _(dve):
            def transform(k, h, c, part):
                d = [xn[c][:, h + j:h + j + 4 * QUADS - 3:4, :] for j in range(6)]
                t = [tmp[i][:] for i in range(4)]
                u = [Uf[c][:, j] for j in range(KW)]
                n = (k * CT + c) * T_STEPS
                stt = nc.vector.scalar_tensor_tensor
                if part == 0:
                    dve.wait_ge(xn_ready[c], k + 1)
                    wait(dve, u_low[c], k * HALVES)
                    wait(dve, u_ready[1 - c], (k + c) * HALVES)
                    stt(t[0], d[2], -4.0, d[4], ALU.mult, ALU.add).then_inc(t_ready, 1)
                    stt(t[1], d[1], -4.0, d[3], ALU.mult, ALU.add).then_inc(t_ready, 1)
                    stt(t[2], d[2], -5.0, d[4], ALU.mult, ALU.add).then_inc(t_ready, 1)
                    dve.wait_ge(t_ready, n + 2)
                    nc.vector.tensor_tensor(u[1], t[0], t[1], ALU.add)
                    nc.vector.tensor_tensor(u[2], t[0], t[1], ALU.subtract)
                    dve.wait_ge(t_ready, n + 3)
                    stt(u[0], d[0], 4.0, t[2], ALU.mult, ALU.add).then_inc(u_ready[c], 1)
                else:
                    stt(t[3], d[3], -5.0, d[5], ALU.mult, ALU.add).then_inc(t_ready, 1)
                    dve.wait_ge(u_ready[c], k * HALVES + 1)
                    nc.vector.tensor_tensor(t[0], d[4], d[2], ALU.subtract).then_inc(t_ready, 1)
                    nc.vector.tensor_tensor(t[1], d[3], d[1], ALU.subtract).then_inc(t_ready, 1)
                    dve.wait_ge(t_ready, n + 6)
                    stt(u[3], t[1], 2.0, t[0], ALU.mult, ALU.add)
                    stt(u[4], t[1], -2.0, t[0], ALU.mult, ALU.add)
                    stt(u[5], d[1], 4.0, t[3], ALU.mult, ALU.add).then_inc(u_ready[c], 1)

            def take_low(k, h, c, half):
                dve.wait_ge(u_high[c], k * HALVES + half + 1)
                ks = slice(half * PER, (half + 1) * PER)
                high, low = (U[h][:, z, c, ks].rearrange("p k y x -> p (k y x)") for z in range(2))
                nc.vector.tensor_tensor(low, Uf[c][:, ks].rearrange("p k y x -> p (k y x)"), high,
                                        ALU.subtract).then_inc(u_low[c], 1)

            def product(h, c, i):
                return slot_bank(h * CT + c, i)[:, 0:N3].rearrange("p (y x) -> p y x", x=W)

            def pair(b, h, c, i):
                g = b * 4 + h * CT + c + 1
                if i == 0 and (before := previous(b, h, c)):
                    dve.wait_ge(y_ready[1 - c], before[0] + 1)
                dve.wait_ge(free[ORDER[i]], g)
                dve.wait_ge(full[ORDER[i + 1]], g)
                a = first[c][i // 2][:]
                nc.vector.tensor_tensor(sums[i // 2][:], a, product(h, c, i + 1), ALU.add)
                nc.vector.tensor_tensor(diffs[i // 2][:], a, product(h, c, i + 1), ALU.subtract
                                        ).then_inc(free[ORDER[i + 1]], 1)

            def rows(b, h, c):
                (p, r), (q, s) = (x[:] for x in sums), (x[:] for x in diffs)
                dve.wait_ge(free[ORDER[3]], b * 4 + h * CT + c + 1)
                wait(dve, rep_ready[c], b * 2 + h)
                stt = nc.vector.scalar_tensor_tensor
                nc.vector.tensor_tensor(y[c][:, :, 0], p, r, ALU.add).then_inc(y_part[c], 1)
                stt(y[c][:, :, 3], s, 8.0, q, ALU.mult, ALU.add).then_inc(y_part[c], 1)
                stt(y[c][:, :, 1], s, 2.0, q, ALU.mult, ALU.add)
                stt(y[c][:, :, 2], r, 4.0, p, ALU.mult, ALU.add)

            def last_rows(b, h, c):
                g = b * 4 + h * CT + c + 1
                dve.wait_ge(y_part[c], (b * 2 + h) * 2 + 2)
                dve.wait_ge(full[0], g)
                nc.vector.tensor_tensor(y[c][:, :, 0], y[c][:, :, 0], product(h, c, 4), ALU.add
                                        ).then_inc(free[0], 1)
                dve.wait_ge(full[5], g)
                nc.vector.tensor_tensor(y[c][:, :, 3], y[c][:, :, 3], product(h, c, 5), ALU.add
                                        ).then_inc(y_ready[c], 1)

            def add_depthwise(k, h, b, c):
                dve.wait_ge(rep_ready[c], k + 1)
                dve.wait_ge(dwt_loaded[c], k * 16 + 16)
                v = rep[c][:].rearrange("p (y x) -> p y x", x=W)
                dwv = dwt[c][:].rearrange("p (y x) -> p y x", x=PITCH)[:, :, 0:W]
                nc.vector.scalar_tensor_tensor(v, dwv, dw_scale[:, c:c + 1], v, ALU.mult, ALU.add
                                               ).then_inc(z_ready[c], 1)

            def prepare_weights():
                done = 0

                def link(ins, hold=True):
                    nonlocal done
                    ins.then_inc(w_step, 1)
                    done += 1
                    if hold:
                        dve.wait_ge(w_step, done)

                v, ts, tt, stt = nc.vector, nc.vector.tensor_scalar, nc.vector.tensor_tensor, \
                    nc.vector.scalar_tensor_tensor
                dve.wait_ge(bn_loaded, 16 * 12)
                var = pn[:, :, 3, :]
                link(ts(var, var, BN_EPS, None, ALU.add))
                dve.wait_ge(bn_sqrt, 1)
                link(v.reciprocal(rs[:], sd[:]))
                link(tt(rt[:], rs[:], rs[:], ALU.mult))
                link(tt(rt[:], rt[:], var, ALU.mult))
                link(ts(rt[:], rt[:], -0.5, 1.5, ALU.mult, ALU.add))
                link(tt(rs[:], rs[:], rt[:], ALU.mult))
                link(tt(fold[:], rs[:], pn[:, :, 0, :], ALU.mult))
                link(tt(pn[:, :, 2, :], pn[:, :, 2, :], fold[:], ALU.mult))
                link(tt(pn[:, :, 1, :], pn[:, :, 1, :], pn[:, :, 2, :], ALU.subtract))
                link(tt(bias1[:], pn[:, 0, 1, :], pn[:, 1, 1, :], ALU.add), False)
                link(v.tensor_copy(bias3[:], pn[:, 2, 1, :]), False)
                link(v.tensor_copy(fold3[:], fold[:, 2, :]), False)
                dve.wait_ge(w_loaded, 32)
                for k in range(CT):
                    link(ts(wn[:, k], wn[:, k], fold[:, 0, k:k + 1], None, ALU.mult))
                    link(stt(wn[:, k, :, 4], wc[:, k], fold[:, 1, k:k + 1], wn[:, k, :, 4], ALU.mult, ALU.add),
                         False)
                dve.wait_ge(w_step, done)
                for k in range(CT):
                    flat = wn[:, k].rearrange("p i t -> p (i t)")
                    one = slice(k, k + 1)
                    link(v.tensor_reduce(wmax[:, one], flat, AXX, ALU.max), False)
                    link(v.tensor_reduce(wmin[:, one], flat, AXX, ALU.min))
                    link(stt(wmax[:, one], wmin[:, one], -1.0, wmax[:, one], ALU.mult, ALU.max))
                    link(ts(wmax[:, one], wmax[:, one], 1e-30, None, ALU.max))
                    link(ts(scale1[:, one], wmax[:, one], 1.0 / (WS * XS), None, ALU.mult), False)
                    link(v.reciprocal(winv[:, one], wmax[:, one]))
                    taps = wn[:, k].rearrange("p i (y x) -> p y x i", x=3)
                    link(ts(wk[:, k, 5], taps[:, 2], winv[:, one], WS, ALU.mult, ALU.mult), False)
                    link(ts(wk[:, k, 0], taps[:, 0], winv[:, one], WS / 4, ALU.mult, ALU.mult), False)
                    link(ts(wh[:], taps[:, 1], winv[:, one], WS / 6, ALU.mult, ALU.mult))
                    link(ts(ws[:], wk[:, k, 5], -1.0 / 6, None, ALU.mult))
                    link(stt(ws[:], wk[:, k, 0], -4.0 / 6, ws[:], ALU.mult, ALU.add))
                    link(tt(wk[:, k, 1], ws[:], wh[:], ALU.subtract), False)
                    link(tt(wk[:, k, 2], ws[:], wh[:], ALU.add))
                    link(ts(ws[:], wk[:, k, 5], 1.0 / 6, None, ALU.mult))
                    link(stt(ws[:], wk[:, k, 0], 1.0 / 6, ws[:], ALU.mult, ALU.add))
                    link(stt(wk[:, k, 3], wh[:], 0.5, ws[:], ALU.mult, ALU.add), False)
                    link(stt(wk[:, k, 4], wh[:], -0.5, ws[:], ALU.mult, ALU.add))
                    assert done == WEIGHT_STEPS[k]

            for c in range(CT):
                for half in range(HALVES):
                    transform(0, 0, c, half)
                for half in range(HALVES):
                    take_low(0, 0, c, half)
            prepare_weights()
            for n, (co, ci, k) in enumerate(BATCHES):
                dve.wait_ge(wt_high[n % 2], n // 2 + 1)
                dst = wt[:, ci, k, :, :, co * P:(co + 1) * P]
                nc.vector.tensor_tensor(dst[:, :, 1], bank[n % 2][:, 0:3 * P].rearrange("p (d m) -> p d m", m=P),
                                        dst[:, :, 0], ALU.subtract).then_inc(wt_low[n % 2], 1)

            def image(b, more):
                for h in range(2):
                    for c in range(CT):
                        prepare = more or h == 0
                        k = b * 2 + h + 1
                        if prepare:
                            transform(k, 1 - h, c, 0)
                        if before := previous(b, h, c):
                            add_depthwise(*before)
                        pair(b, h, c, 0)
                        if prepare:
                            transform(k, 1 - h, c, 1)
                            take_low(k, 1 - h, c, 0)
                        pair(b, h, c, 2)
                        rows(b, h, c)
                        if prepare:
                            take_low(k, 1 - h, c, 1)
                        last_rows(b, h, c)
            images(dve, image)
            add_depthwise(2 * B - 1, 1, B - 1, 1)


_NAMES = ["x"] + ["L0_conv_" + n for n in ("w3", "g1", "b1", "m1", "v1", "w1", "g2", "b2", "m2", "v2",
                                           "dw7", "dwk", "g3", "b3", "m3", "v3")]


def kernel(**inputs):
    import numpy as _np
    import concourse.bacc as _bacc
    from concourse import mybir as _mybir
    from concourse.bass_utils import run_bass_kernel_spmd as _run

    nc = _bacc.Bacc("TRN2", target_bir_lowering=False, num_devices=1)
    arrays, args = {}, []
    p = _np.arange(P)
    consts = {
        "ident": _np.eye(P, dtype=_np.float32),
        "gmat": ((p[:, None] // (GROUP_C * BH) == p[None, :] // (GROUP_C * BH))
                 & (p[:, None] % BH == p[None, :] % BH)).astype(_np.float32) / _np.float32(GROUP_C),
    }
    for name in _NAMES + list(consts):
        a = _np.ascontiguousarray(inputs[name] if name in inputs else consts[name])
        arrays[f"in_{name}"] = a
        args.append(nc.dram_tensor(f"in_{name}", a.shape, _mybir.dt.from_np(a.dtype), kind="ExternalInput").ap())
    args.append(nc.dram_tensor("out_0", (B, C, H, W), F32, kind="ExternalOutput").ap())
    build(nc, *args)
    r = _run(nc, [arrays], core_ids=[0])
    return r.results[0]["out_0"]
```

```python
from contextlib import ExitStack

import numpy as np
import concourse.bass as bass
from concourse import mybir

F32 = mybir.dt.float32
F16 = mybir.dt.float16
ALU = mybir.AluOpType
ACT = mybir.ActivationFunctionType
AXX = mybir.AxisListType.X

P = 128
B, C, H, W = 16, 256, 56, 56
HW = H * W
CT = C // P
GROUP_C = C // 32
GN_EPS = 1e-5
BN_EPS = 1e-5
XS = 32.0
WS = 256.0

K7 = 7
R7 = K7 // 2
STRIPS = 4
SW = W // STRIPS
PITCH = SW + 2 * R7
STRIP_PITCH = (H + R7) * PITCH
REACH = R7 * PITCH + R7
OUT_BLOCKS = -(-((STRIPS - 1) * STRIP_PITCH + PITCH * (H - 1) + SW) // P)
TAP_BLOCKS = 2
assert P + 2 * REACH <= TAP_BLOCKS * P
LEAD = REACH
IN_BLOCKS = OUT_BLOCKS + 1
STRIP = TAP_BLOCKS * P
VEC = STRIP + P
CC = GROUP_C
assert CC * B == P
CHUNKS = C // CC
BH = B // 2
IN_BATCHES = -(-IN_BLOCKS // 4)
OUT_BATCHES = -(-OUT_BLOCKS // 4)

KW = 6
WPAD = W + 2
STEP_ROWS = H // 2
X_ROWS = STEP_ROWS + 1
QUADS = STEP_ROWS // 4
N3 = QUADS * W
NT = STEP_ROWS * W

LOW_SIZE = CT * KW * 3 * C + CT * X_ROWS * W
HIGH_SIZE = 4 * CT * NT + 3 * CT * KW * QUADS * WPAD + 2 * N3


def strip_centre():
    return LEAD + P - 1


def build(nc, x, w3, g1, b1, m1, v1, w1, g2, b2, m2, v2, dw7, dwk, g3, b3, m3, v3, ident_d, gmat_d, out):
    root = ExitStack()

    def sb(ctx, name, shape, dt=F32):
        return ctx.enter_context(nc.sbuf_tensor(name, shape, dt))

    def sem(name):
        return root.enter_context(nc.semaphore(name))

    x3 = x.rearrange("b c h w -> b c (h w)")
    out3 = out.rearrange("b c h w -> b c (h w)")
    vec_d = nc.dram_tensor("strip_vectors", [C, 2, VEC], F16, kind="Internal").ap()
    dw_d = nc.dram_tensor("depthwise_out", [B, C, HW], F32, kind="Internal").ap()
    st_d = nc.dram_tensor("gn_stats", [B, C, 2], F32, kind="Internal").ap()

    with root:
        pair = [root.enter_context(nc.psum_tensor(f"pair{i}", [P, 1024], F32)) for i in range(2)]
        bank = [root.enter_context(nc.psum_tensor(f"bank{i}", [P, 512], F32)) for i in (0, 1, 6, 7)]
        bank[2:2] = [pair[i][:, h * 512:(h + 1) * 512] for i in range(2) for h in range(2)]
        mem = Memory()
        mem.ident = sb(root, "ident", [P, P])
        mem.dw_scale = sb(root, "dw_scale", [P, CT])
        mem.scale1 = sb(root, "scale1", [P, CT])
        mem.bias1 = sb(root, "bias1", [P, CT])
        mem.fold3 = sb(root, "fold3", [P, CT])
        mem.bias3 = sb(root, "bias3", [P, CT])
        mem.stp = [sb(root, f"stp{h}", [P, CT, 2]) for h in range(2)]
        mem.mid = sb(root, "mid", [P, 2 * HW + IN_BLOCKS * P])
        mem.low = sb(root, "low", [P, LOW_SIZE])
        mem.high = sb(root, "high", [P, HIGH_SIZE])
        mem.wt, at = view(mem.low, 0, [CT, KW, 3, 2, C], F16)
        mem.X = [view(mem.low, at, [CT, X_ROWS, W])[0], view(mem.mid, 0, [CT, X_ROWS, W])[0]]
        at, mem.xn = CT * X_ROWS * W, []
        for c in range(CT):
            t, at = view(mem.mid, at, [STEP_ROWS + 3, WPAD])
            mem.xn.append(t)
        mem.mid_used = at
        mem.pad_zero = sem("dense_padding_zeroed")
        mem.xn_ready = [sem(f"xn_ready{c}") for c in range(CT)]
        mem.first_loaded = [sem(f"first_image_loaded{h}") for h in range(2)]
        mem.o_stored = [sem(f"depthwise_stored{s}") for s in range(2)]
        weights = (w3, w1, (g1, b1, m1, v1), (g2, b2, m2, v2), (g3, b3, m3, v3))
        depthwise(nc, sb, sem, bank, pair, mem, weights, ident_d, dw7, dwk, x3, vec_d, dw_d, st_d, gmat_d)
        dense(nc, sb, sem, bank, mem, x3, dw_d, st_d, out3)
    return nc


class Memory:
    pass


def view(region, at, shape, dt=F32):
    n = int(np.prod(shape)) // (1 if dt == F32 else 2)
    flat = region[:, at:at + n]
    if dt != F32:
        flat = flat.bitcast(dt)
    names = "abcdef"[:len(shape)]
    if len(shape) > 1:
        flat = flat.rearrange(f"p ({' '.join(names)}) -> p {' '.join(names)}", **dict(zip(names, shape)))
    return flat, at + n


def half_image(x3, st_d, b, h):
    r = 0 if h == 0 else STEP_ROWS - 1
    rows = x3[bass.ds(b, 1), :, r * W:(r + X_ROWS) * W].rearrange("a (k p) q -> p k (a q)", p=P)
    return rows, st_d[bass.ds(b, 1)].rearrange("a (k p) v -> p k (a v)", p=P)


def wait(eng, sem, value):
    if not isinstance(value, int) or value > 0:
        eng.wait_ge(sem, value)


def depthwise(nc, sb, sem, bank, pair, mem, weights, ident_d, dw7, dwk, x3, vec_d, dw_d, st_d, gmat_d):
    T, BK = bank[0:2], bank[6:8]
    GS = T[0]
    w3, w1, bn1, bn2, bn3 = weights
    ident, dw_scale = mem.ident, mem.dw_scale
    with ExitStack() as ctx:
        gmat = sb(ctx, "gmat", [P, P])
        Xa = [mem.mid[:, s * HW:(s + 1) * HW] for s in range(2)]
        Xp = mem.mid[:, 2 * HW:2 * HW + IN_BLOCKS * P]
        ws, at = view(mem.mid, 0, [3, C])
        wh, at = view(mem.mid, at, [3, C])
        wk, _ = view(mem.mid, at, [CT, KW, 3, C])
        assert at + KW * 3 * C <= 2 * HW
        wn, at = view(mem.low, 0, [CT, C, 9])
        wc, at = view(mem.low, at, [CT, C])
        d_shape, s_shape = [2, 2 * CC, IN_BLOCKS * BH], [CC, 2, STRIP]
        d0, at = view(mem.low, at, d_shape, F16)
        s0, _ = view(mem.low, at, s_shape, F16)
        wt = mem.wt
        at, Oc = 0, []
        for s in range(2):
            t, at = view(mem.high, at, [HW])
            Oc.append(t)
        d1, at = view(mem.high, at, d_shape, F16)
        s1, at = view(mem.high, at, s_shape, F16)
        D, S, Y = [d0, d1], [s0, s1], []
        O, at = view(mem.high, at, [OUT_BLOCKS * P])
        y_at = at
        for s in range(2):
            t, at = view(mem.high, at, [OUT_BLOCKS, P])
            Y.append(t)
        dwa, at = view(mem.high, y_at, [CT, K7 * K7])
        dwb, at = view(mem.high, at, [CT, K7 * K7])
        vec, at = view(mem.high, at, [CT, VEC])
        vech, _ = view(mem.high, at, [CT, 2, VEC], F16)
        dmax, dmin, dinv = (sb(ctx, n, [P, CT]) for n in ("dmax", "dmin", "dinv"))
        pn = sb(ctx, "pn", [P, 3, 4, CT])
        sd, rs, rt, fold = (sb(ctx, n, [P, 3, CT]) for n in ("sd", "rs", "rt", "fold"))
        wmax, wmin, winv = (sb(ctx, n, [P, CT]) for n in ("wmax", "wmin", "winv"))
        bn = sb(ctx, "bn", [P, 7, 6])
        mv = sb(ctx, "mv", [P, 2])
        dev = sb(ctx, "dev", [P, 2])
        var, std, neg = (sb(ctx, n, [P, 1]) for n in ("var", "std", "neg"))
        newton = sb(ctx, "newton", [P, 3])
        st = [sb(ctx, f"st{s}", [P, 2]) for s in range(2)]
        unit = sb(ctx, "unit", [P, 1])

        s_unit = sem("unit_set")
        s_const, s_zero = sem("constants_loaded"), sem("padding_zeroed")
        s_dw, s_filter, s_vec = sem("dw_loaded"), sem("filter_steps"), sem("vectors_stored")
        w_loaded, bn_loaded = sem("w_loaded"), sem("bn_loaded")
        w_step, bn_sqrt = sem("weight_steps"), sem("bn_sqrt")
        wt_full = [sem(f"wt_full{i}") for i in range(2)]
        wt_high = [sem(f"wt_high{i}") for i in range(2)]
        wt_low = [sem(f"wt_low{i}") for i in range(2)]
        xa_loaded = [sem(f"xa_loaded{s}") for s in range(2)]
        xp_ready = sem("xp_ready")
        t_full = [sem(f"t_full{i}") for i in range(2)]
        t_high = [sem(f"t_high{i}") for i in range(2)]
        t_low = [sem(f"t_low{i}") for i in range(2)]
        s_loaded = [sem(f"s_loaded{s}") for s in range(2)]
        cv_full = [sem(f"cv_full{i}") for i in range(2)]
        cv_free = [sem(f"cv_free{i}") for i in range(2)]
        bk_full, bk_free = sem("bk_full"), sem("bk_free")
        packed, last_packed = sem("packed"), sem("last_packed")
        o_stored = mem.o_stored
        st_stored = [sem(f"st_stored{s}") for s in range(2)]
        q_pieces, q_aggr, q_gmean = sem("bn_pieces"), sem("bn_aggr"), sem("group_mean")
        q_diff, q_dev, q_gvar = sem("mean_diff"), sem("deviation"), sem("group_var")
        q_var, q_newton = sem("group_var_scaled"), sem("rsqrt_steps")
        q_std, q_rstd = sem("group_std"), sem("group_rstd")

        def chunks(eng, step):
            for n in range(4):
                step(n, n // 2, n % 2)
            with eng.Fori(2, CHUNKS // 2 - 2) as m:
                step(m * 2, m, 0)
                step(m * 2 + 1, m, 1)
            for n in range(CHUNKS - 4, CHUNKS):
                step(n, n // 2, n % 2)

        def has(n, last):
            return not isinstance(n, int) or n <= last

        def is_step(n, k):
            return isinstance(n, int) and n == k

        def blocks_of(k, count):
            return range(4 * k, min(4 * k + 4, count))

        SLOTS = 2 * CC
        OUT_AT = SLOTS - OUT_BATCHES
        PIECES = 7
        strip_at = [min(STRIPS - 1, (512 * k + 511) // STRIP_PITCH) for k in range(OUT_BATCHES)]
        strip_in = [min(STRIPS - 1, (512 * k + 511 - LEAD + R7) // STRIP_PITCH) for k in range(IN_BATCHES)]
        batch_of = [(s * STRIP_PITCH + (H - 1) * PITCH + SW - 1) // 512 for s in range(STRIPS)]

        BATCHES = [(co, ci, k) for co in range(CT) for k in range(KW) for ci in range(CT)]
        WT_AT = SLOTS - len(BATCHES) // 2
        BN_STEPS = 12
        WEIGHT_STEPS = BN_STEPS + (8 + 11) * CT
        FILTER_STEPS = 11

        block = ctx.enter_context(nc.Block())

        @block.gpsimd
        def _(pool):
            def load_x(n, m, s):
                wait(pool, xp_ready, (n - 1) * STRIPS)
                src = x3[:, bass.ds(n * CC, CC), :].rearrange("b c q -> c b q")
                pool.dma_start(Xa[s], src).then_inc(xa_loaded[s], 16)

            nc.gpsimd.memset(unit[:], 1.0).then_inc(s_unit, 1)
            ones = unit[:].unsqueeze(2).to_broadcast([P, H, SW])
            pool.wait_ge(s_unit, 1)

            def pack(n, m, s):
                for k in range(STRIPS):
                    if k == 0:
                        wait(pool, o_stored[s], m * 16)
                    pool.wait_ge(bk_free, n * OUT_BATCHES + batch_of[k] + 1)
                    at = k * STRIP_PITCH
                    src = O[:, at:at + H * PITCH].rearrange("p (y x) -> p y x", x=PITCH)[:, :, 0:SW]
                    dst = Oc[s].rearrange("p (y x) -> p y x", x=W)[:, :, k * SW:(k + 1) * SW]
                    nc.gpsimd.tensor_tensor(dst, src, ones, ALU.mult).then_inc(packed, 1)

            for s in range(2):
                pool.dma_start(Xa[s], x3[:, s * CC:(s + 1) * CC, :].rearrange("b c q -> c b q")
                               ).then_inc(xa_loaded[s], 16)
            nc.gpsimd.memset(Xp, 0.0).then_inc(s_zero, 1)
            for s in range(2):
                load_x(2 + s, 1, s)

            def step(n, m, s):
                if not is_step(n, 0):
                    pack(n - 1, m - 1 + s, 1 - s)
                if has(n, CHUNKS - 5):
                    load_x(n + 4, m + 2, s)

            chunks(pool, step)
            for i in range(2):
                pool.wait_ge(wt_full[i], len(BATCHES) // 2)
            for t in mem.xn:
                nc.gpsimd.memset(t[:, 0:STEP_ROWS + 3:STEP_ROWS + 2, :], 0.0).then_inc(mem.pad_zero, 1)
                nc.gpsimd.memset(t[:, 1:X_ROWS + 1, 0:WPAD:WPAD - 1], 0.0).then_inc(mem.pad_zero, 1)

        @block.sync
        def _(sp):
            with nc.allow_non_contiguous_dma(reason="small"):
                sp.dma_start(dwa, dw7.rearrange("(k p) o y x -> p k (o y x)", p=P)).then_inc(s_dw, 16)
                sp.dma_start(dwb, dwk.rearrange("(k p) o y x -> p k (o y x)", p=P)).then_inc(s_dw, 16)
            sp.dma_start(gmat[:], gmat_d).then_inc(s_const, 16)
            sp.dma_start(ident[:], ident_d).then_inc(s_const, 16)
            sp.wait_ge(s_filter, FILTER_STEPS)
            for k in range(CT):
                sp.dma_start(vec_d[k * P:(k + 1) * P], vech[:, k]).then_inc(s_vec, 16)
            sp.wait_ge(s_vec, 16 * CT)

            def load_strips(n, s):
                v = vec_d[bass.ds(n * CC, CC)]
                src = bass.AP(v.tensor, v.offset, [[1, P], [VEC, CC * 2], [1, STRIP]])
                sp.dma_start(S[s].rearrange("p c z m -> p (c z) m"), src).then_inc(s_loaded[s], 16)

            def store_stats(n, s):
                sp.wait_ge(q_rstd, n + 1)
                dst = st_d[:, bass.ds(n * CC, CC), :].rearrange("b c v -> c b v")
                sp.dma_start(dst, st[s][:]).then_inc(st_stored[s], 16)

            def store_out(n, s):
                if is_step(n, CHUNKS - 1):
                    sp.wait_ge(last_packed, STRIPS)
                else:
                    sp.wait_ge(packed, n * STRIPS + STRIPS)
                dst = dw_d[:, bass.ds(n * CC, CC), :].rearrange("b c q -> c b q")
                sp.dma_start(dst, Oc[s]).then_inc(o_stored[s], 16)

            for s in range(2):
                load_strips(s, s)
            with nc.allow_non_contiguous_dma(reason="one value per channel"):
                for i, bns in enumerate((bn1, bn2, bn3)):
                    for j, a in enumerate(bns):
                        sp.dma_start(pn[:, i, j, :], a.rearrange("(k p) -> p k", p=P)).then_inc(bn_loaded, 16)
            for s in range(2):
                store_stats(s, s)
            sp.dma_start(wn.rearrange("p k i t -> p k (i t)"),
                         w3.rearrange("(k p) i y x -> p k (i y x)", p=P)).then_inc(w_loaded, 16)
            sp.dma_start(wc, w1.rearrange("(k p) i y x -> p k (i y x)", p=P)).then_inc(w_loaded, 16)

            def first_half(h):
                rows, stats = half_image(x3, st_d, 0, h)
                sp.dma_start(mem.X[h].rearrange("p k y x -> p k (y x)"), rows
                             ).then_inc(mem.first_loaded[h], 16)
                sp.dma_start(mem.stp[h][:], stats).then_inc(mem.first_loaded[h], 16)

            def step(n, m, s):
                if is_step(n, CHUNKS - 1):
                    sp.wait_ge(cv_full[1], (CHUNKS - 1) * CC // 2)
                    for i in range(2):
                        sp.wait_ge(st_stored[i], 16 * CHUNKS // 2)
                    first_half(0)
                if has(n, CHUNKS - 3):
                    store_stats(n + 2, s)
                    sp.wait_ge(cv_full[1], (n + 1) * (CC // 2))
                    load_strips(n + 2, s)
                if not is_step(n, 0):
                    store_out(n - 1, 1 - s)

            chunks(sp, step)
            for i in range(2):
                sp.wait_ge(wt_full[i], len(BATCHES) // 2)
            first_half(1)
            store_out(CHUNKS - 1, 1)

        @block.tensor
        def _(pe):
            def group_mean(n):
                wait(pe, t_low[0], n * (IN_BATCHES // 2))
                pe.wait_ge(q_aggr, n + 1)
                nc.tensor.matmul(GS[:, 0:1], gmat[:], mv[:, 0:1], start=True, stop=True).then_inc(q_gmean, 1)

            def group_var(n):
                pe.wait_ge(q_dev, n + 1)
                nc.tensor.matmul(GS[:, 1:2], gmat[:], dev[:, 1:2], start=True, stop=True).then_inc(q_gvar, 1)

            def transpose_in(n, k):
                if k == 0:
                    pe.wait_ge(q_var, n + 1)
                if k == 0 or strip_in[k] > strip_in[k - 1]:
                    pe.wait_ge(xp_ready, n * STRIPS + strip_in[k] + 1)
                wait(pe, t_low[k % 2], n * (IN_BATCHES // 2) + k // 2)
                for j, b in enumerate(blocks_of(k, IN_BLOCKS)):
                    last = nc.tensor.transpose(T[k % 2][:, j * P:(j + 1) * P], Xp[:, b * P:(b + 1) * P], ident[:])
                last.then_inc(t_full[k % 2], 1)

            def transpose_out(n, s, k):
                if k == 0:
                    for i in range(2):
                        pe.wait_ge(cv_free[i], (n + 1) * (CC // 2))
                wait(pe, bk_free, n * OUT_BATCHES + k - 1)
                for j, b in enumerate(blocks_of(k, OUT_BLOCKS)):
                    last = nc.tensor.transpose(BK[k % 2][:, j * P:(j + 1) * P], Y[s][:, b, :], ident[:])
                last.then_inc(bk_full, 1)

            def convolve(n, s, c, h):
                if c == 0 and h == 0:
                    for i in range(2):
                        pe.wait_ge(t_low[i], (n + 1) * (IN_BATCHES // 2))
                    pe.wait_ge(s_loaded[s], (n - s) * 8 + 16)
                if h == 0:
                    wait(pe, cv_free[c % 2], n * (CC // 2) + c // 2)
                acc = pair[c % 2][:, h * 512:h * 512 + OUT_BLOCKS * BH]
                for z, (hs, hd) in enumerate(((0, 0), (0, 1), (1, 0))):
                    for j in range(TAP_BLOCKS):
                        last = nc.tensor.matmul(
                            acc, S[s][:, c, hs, j * P:(j + 1) * P],
                            D[s][:, hd, 2 * c + h, j * BH:(j + OUT_BLOCKS) * BH],
                            start=(z == 0 and j == 0), stop=(z == 2 and j == TAP_BLOCKS - 1))
                if h == 1:
                    last.then_inc(cv_full[c % 2], 1)

            def weights_batch(n):
                co, ci, k = BATCHES[n]
                if n == 0:
                    pe.wait_ge(w_step, WEIGHT_STEPS)
                pe.wait_ge(t_low[n % 2], CHUNKS * (IN_BATCHES // 2))
                wait(pe, wt_low[n % 2], n // 2)
                for d in range(3):
                    last = nc.tensor.transpose(T[n % 2][:, d * P:(d + 1) * P],
                                               wk[:, co, k, d, ci * P:(ci + 1) * P], ident[:])
                last.then_inc(wt_full[n % 2], 1)

            pe.wait_ge(s_const, 32)
            group_mean(0)
            group_var(0)
            for k in range(IN_BATCHES):
                transpose_in(0, k)
            group_mean(1)
            group_var(1)

            def step(n, m, s):
                for j in range(SLOTS):
                    convolve(n, s, j // 2, j % 2)
                    if not is_step(n, 0) and j >= OUT_AT:
                        transpose_out(n - 1, 1 - s, j - OUT_AT)
                    if has(n, CHUNKS - 2) and j < IN_BATCHES:
                        transpose_in(n + 1, j)
                    if has(n, CHUNKS - 3):
                        if j == 10:
                            group_mean(n + 2)
                        if j == 12:
                            group_var(n + 2)
                    if is_step(n, CHUNKS - 1) and j >= WT_AT:
                        for i in range(2):
                            weights_batch(2 * (j - WT_AT) + i)

            chunks(pe, step)
            for k in range(OUT_BATCHES):
                transpose_out(CHUNKS - 1, 1, k)

        @block.scalar
        def _(act):
            def take_high(n, s, k):
                nb = len(blocks_of(k, IN_BLOCKS))
                act.wait_ge(t_full[k % 2], n * (IN_BATCHES // 2) + k // 2 + 1)
                dst = D[s][:, 0, :, 4 * k * BH:(4 * k + nb) * BH].rearrange("p g (k b) -> p k g b", b=BH)
                src = T[k % 2][:, 0:nb * P].rearrange("p (k g b) -> p k g b", g=2 * CC, b=BH)
                nc.scalar.copy(dst, src).then_inc(t_high[k % 2], 1)

            def take_conv(n, s, c):
                act.wait_ge(cv_full[c % 2], n * (CC // 2) + c // 2 + 1)
                dst = Y[s][:, :, c * B:(c + 1) * B].rearrange("p k (h b) -> p h k b", b=BH)
                src = pair[c % 2][:].rearrange("p (h q) -> p h q", h=2)[:, :, 0:OUT_BLOCKS * BH]
                nc.scalar.copy(dst, src.rearrange("p h (k b) -> p h k b", b=BH)).then_inc(cv_free[c % 2], 1)

            def take_out(n, k):
                if k == 0 or strip_at[k] > strip_at[k - 1]:
                    wait(act, packed, n * STRIPS - STRIPS + strip_at[k] + 1)
                act.wait_ge(bk_full, n * OUT_BATCHES + k + 1)
                blocks = blocks_of(k, OUT_BLOCKS)
                dst = O[:, blocks[0] * P:(blocks[-1] + 1) * P].rearrange("p (k m) -> p k m", m=P)
                src = BK[k % 2][:, 0:len(blocks) * P].rearrange("p (k m) -> p k m", m=P)
                nc.scalar.copy(dst, src[:, :, ::-1]).then_inc(bk_free, 1)

            def group_std(n):
                act.wait_ge(q_var, n + 1)
                nc.scalar.activation(std[:], var[:], ACT.Sqrt).then_inc(q_std, 1)

            def weights_high(n):
                co, ci, k = BATCHES[n]
                act.wait_ge(wt_full[n % 2], n // 2 + 1)
                nc.scalar.copy(wt[:, ci, k, :, 0, co * P:(co + 1) * P],
                               T[n % 2][:, 0:3 * P].rearrange("p (d m) -> p d m", m=P)).then_inc(wt_high[n % 2], 1)

            group_std(0)
            for k in range(IN_BATCHES):
                take_high(0, 0, k)
            group_std(1)
            act.wait_ge(w_step, 1)
            nc.scalar.activation(sd[:], pn[:, :, 3, :], ACT.Sqrt).then_inc(bn_sqrt, 1)
            act.wait_ge(s_vec, 16 * CT)

            def step(n, m, s):
                for j in range(SLOTS):
                    if j % 2 == 1:
                        take_conv(n, s, j // 2)
                    if not is_step(n, 0) and j >= OUT_AT:
                        take_out(n - 1, j - OUT_AT)
                    if has(n, CHUNKS - 2) and j < IN_BATCHES:
                        take_high(n + 1, 1 - s, j)
                    if has(n, CHUNKS - 3) and j == 12:
                        group_std(n + 2)
                    if is_step(n, CHUNKS - 1) and j >= WT_AT:
                        for i in range(2):
                            weights_high(2 * (j - WT_AT) + i)

            chunks(act, step)
            for k in range(OUT_BATCHES):
                take_out(CHUNKS - 1, k)

        @block.vector
        def _(dve):
            def stat_piece(n, m, s, k):
                if k == 0:
                    dve.wait_ge(xa_loaded[s], m * 16 + 16)
                size = HW // PIECES
                nc.vector.bn_stats(bn[:, k, :], Xa[s][:, k * size:(k + 1) * size]).then_inc(q_pieces, 1)

            def stat_pieces_done(n):
                dve.wait_ge(q_pieces, (n + 1) * PIECES)

            def stat_aggregate(n):
                nc.vector.bn_aggr(mv[:], bn[:].rearrange("p k v -> p (k v)")).then_inc(q_aggr, 1)

            def stat_deviation(n, m, s):
                dve.wait_ge(q_gmean, n + 1)
                wait(dve, st_stored[s], m * 16)
                wait(dve, xp_ready, n * STRIPS)
                nc.vector.tensor_scalar(neg[:], GS[:, 0:1], -1.0, None, ALU.mult)
                nc.vector.tensor_tensor(dev[:, 0:1], mv[:, 0:1], GS[:, 0:1], ALU.subtract).then_inc(q_diff, 1)
                dve.wait_ge(q_diff, n + 1)
                nc.vector.scalar_tensor_tensor(dev[:, 1:2], dev[:, 0:1], dev[:, 0:1], mv[:, 1:2],
                                               ALU.mult, ALU.add).then_inc(q_dev, 1)

            def stat_variance(n):
                dve.wait_ge(q_gvar, n + 1)
                nc.vector.tensor_scalar(var[:], GS[:, 1:2], GN_EPS, 1.0 / (XS * XS),
                                        ALU.add, ALU.mult).then_inc(q_var, 1)

            def stat_scale(n, s):
                r, t, u = (newton[:, i:i + 1] for i in range(3))
                dve.wait_ge(q_std, n + 1)
                nc.vector.reciprocal(r, std[:]).then_inc(q_newton, 1)
                dve.wait_ge(q_newton, n * 4 + 1)
                nc.vector.scalar_tensor_tensor(t, r, r, var[:], ALU.mult, ALU.mult).then_inc(q_newton, 1)
                dve.wait_ge(q_newton, n * 4 + 2)
                nc.vector.tensor_scalar(u, t, -0.5, 1.5, ALU.mult, ALU.add).then_inc(q_newton, 1)
                dve.wait_ge(q_newton, n * 4 + 3)
                nc.vector.tensor_tensor(st[s][:, 1:2], r, u, ALU.mult).then_inc(q_newton, 1)
                dve.wait_ge(q_newton, n * 4 + 4)
                nc.vector.tensor_tensor(st[s][:, 0:1], neg[:], st[s][:, 1:2], ALU.mult).then_inc(q_rstd, 1)

            def normalise(n, s, k):
                if k == 0 and not is_step(n, 0):
                    dve.wait_ge(t_full[(IN_BATCHES - 1) % 2], n * (IN_BATCHES // 2))
                lo, hi = max(0, k * SW - R7), min(W, (k + 1) * SW + R7)
                skip = lo - (k * SW - R7)
                at = LEAD - R7 + k * STRIP_PITCH
                dst = Xp[:, at:at + H * PITCH].rearrange("p (y x) -> p y x", x=PITCH)[:, :, skip:skip + hi - lo]
                src = Xa[s].rearrange("p (y x) -> p y x", x=W)[:, :, lo:hi]
                nc.vector.tensor_scalar(dst, src, neg[:], st[s][:, 1:2], ALU.add, ALU.mult).then_inc(xp_ready, 1)

            def take_low(n, s, k):
                nb = len(blocks_of(k, IN_BLOCKS))
                dve.wait_ge(t_high[k % 2], n * (IN_BATCHES // 2) + k // 2 + 1)
                high, low = (D[s][:, z, :, 4 * k * BH:(4 * k + nb) * BH].rearrange("p g (k b) -> p k g b", b=BH)
                             for z in range(2))
                src = T[k % 2][:, 0:nb * P].rearrange("p (k g b) -> p k g b", g=2 * CC, b=BH)
                nc.vector.tensor_tensor(low, src, high, ALU.subtract).then_inc(t_low[k % 2], 1)

            def prepare_filters():
                done = 0

                def link(ins, hold=True):
                    nonlocal done
                    ins.then_inc(s_filter, 1)
                    done += 1
                    if hold:
                        dve.wait_ge(s_filter, done)

                link(nc.vector.memset(vec, 0.0), False)
                dve.wait_ge(s_dw, 32)
                link(nc.vector.tensor_tensor(dwa, dwa, dwb, ALU.add))
                link(nc.vector.tensor_reduce(dmax[:], dwa, AXX, ALU.max), False)
                link(nc.vector.tensor_reduce(dmin[:], dwa, AXX, ALU.min))
                link(nc.vector.scalar_tensor_tensor(dmax[:], dmin[:], -1.0, dmax[:], ALU.mult, ALU.max))
                link(nc.vector.tensor_scalar(dmax[:], dmax[:], 1e-30, None, ALU.max))
                nc.vector.tensor_scalar(dw_scale[:], dmax[:], 1.0 / (WS * XS), None, ALU.mult)
                link(nc.vector.reciprocal(dinv[:], dmax[:]))
                at = strip_centre() - REACH
                for k in range(CT):
                    rows = vec[:, k, at:at + K7 * PITCH].rearrange("p (y x) -> p y x", x=PITCH)[:, :, 0:K7]
                    link(nc.vector.tensor_scalar(rows, dwa[:, k, :].rearrange("p (y x) -> p y x", x=K7),
                                                 dinv[:, k:k + 1], WS, ALU.mult, ALU.mult), k == CT - 1)
                link(nc.vector.tensor_copy(vech[:, :, 0, :], vec))
                link(nc.vector.tensor_tensor(vech[:, :, 1, :], vec, vech[:, :, 0, :], ALU.subtract), False)
                assert done == FILTER_STEPS

            done = 0
            v, ts, tt, stt = nc.vector, nc.vector.tensor_scalar, nc.vector.tensor_tensor, \
                nc.vector.scalar_tensor_tensor

            def link(ins, hold=True):
                nonlocal done
                ins.then_inc(w_step, 1)
                done += 1
                if hold:
                    dve.wait_ge(w_step, done)

            def bn_variance():
                dve.wait_ge(bn_loaded, 16 * 12)
                link(ts(pn[:, :, 3, :], pn[:, :, 3, :], BN_EPS, None, ALU.add), False)

            def prepare_bn():
                var = pn[:, :, 3, :]
                dve.wait_ge(bn_sqrt, 1)
                link(v.reciprocal(rs[:], sd[:]))
                link(tt(rt[:], rs[:], rs[:], ALU.mult))
                link(tt(rt[:], rt[:], var, ALU.mult))
                link(ts(rt[:], rt[:], -0.5, 1.5, ALU.mult, ALU.add))
                link(tt(rs[:], rs[:], rt[:], ALU.mult))
                link(tt(fold[:], rs[:], pn[:, :, 0, :], ALU.mult))
                link(tt(pn[:, :, 2, :], pn[:, :, 2, :], fold[:], ALU.mult))
                link(tt(pn[:, :, 1, :], pn[:, :, 1, :], pn[:, :, 2, :], ALU.subtract))
                link(tt(mem.bias1[:], pn[:, 0, 1, :], pn[:, 1, 1, :], ALU.add), False)
                link(v.tensor_copy(mem.bias3[:], pn[:, 2, 1, :]), False)
                link(v.tensor_copy(mem.fold3[:], fold[:, 2, :]), False)
                assert done == BN_STEPS

            def scale_weights(k, part):
                flat = wn[:, k].rearrange("p i t -> p (i t)")
                one = slice(k, k + 1)
                if part == 0:
                    dve.wait_ge(w_loaded, 32)
                    link(ts(wn[:, k], wn[:, k], fold[:, 0, k:k + 1], None, ALU.mult))
                    link(stt(wn[:, k, :, 4], wc[:, k], fold[:, 1, k:k + 1], wn[:, k, :, 4], ALU.mult, ALU.add))
                if part == 1:
                    link(v.tensor_reduce(wmax[:, one], flat, AXX, ALU.max), False)
                if part == 2:
                    link(v.tensor_reduce(wmin[:, one], flat, AXX, ALU.min))
                    link(stt(wmax[:, one], wmin[:, one], -1.0, wmax[:, one], ALU.mult, ALU.max))
                    link(ts(wmax[:, one], wmax[:, one], 1e-30, None, ALU.max))
                    link(ts(mem.scale1[:, one], wmax[:, one], 1.0 / (WS * XS), None, ALU.mult), False)
                    link(v.reciprocal(winv[:, one], wmax[:, one]))

            def transform_weights(k, part):
                one = slice(k, k + 1)
                taps = wn[:, k].rearrange("p i (y x) -> p y x i", x=3)
                if k == 0 and part == 0:
                    dve.wait_ge(xp_ready, CHUNKS * STRIPS)
                if part == 0:
                    link(ts(wk[:, k, 5], taps[:, 2], winv[:, one], WS, ALU.mult, ALU.mult), False)
                    link(ts(wk[:, k, 0], taps[:, 0], winv[:, one], WS / 4, ALU.mult, ALU.mult), False)
                if part == 1:
                    link(ts(wh, taps[:, 1], winv[:, one], WS / 6, ALU.mult, ALU.mult))
                    link(ts(ws, wk[:, k, 5], -1.0 / 6, None, ALU.mult))
                if part == 2:
                    link(stt(ws, wk[:, k, 0], -4.0 / 6, ws, ALU.mult, ALU.add))
                    link(tt(wk[:, k, 1], ws, wh, ALU.subtract), False)
                    link(tt(wk[:, k, 2], ws, wh, ALU.add))
                if part == 3:
                    link(ts(ws, wk[:, k, 5], 1.0 / 6, None, ALU.mult))
                    link(stt(ws, wk[:, k, 0], 1.0 / 6, ws, ALU.mult, ALU.add))
                if part == 4:
                    link(stt(wk[:, k, 3], wh, 0.5, ws, ALU.mult, ALU.add), False)
                    link(stt(wk[:, k, 4], wh, -0.5, ws, ALU.mult, ALU.add))

            def weights_low(n):
                co, ci, k = BATCHES[n]
                dve.wait_ge(wt_high[n % 2], n // 2 + 1)
                dst = wt[:, ci, k, :, :, co * P:(co + 1) * P]
                nc.vector.tensor_tensor(dst[:, :, 1], T[n % 2][:, 0:3 * P].rearrange("p (d m) -> p d m", m=P),
                                        dst[:, :, 0], ALU.subtract).then_inc(wt_low[n % 2], 1)

            prepare_filters()
            for k in range(PIECES):
                stat_piece(0, 0, 0, k)
            stat_pieces_done(0)
            stat_aggregate(0)
            stat_deviation(0, 0, 0)
            stat_variance(0)
            stat_scale(0, 0)
            dve.wait_ge(s_zero, 1)
            for k in range(STRIPS):
                normalise(0, 0, k)
            for k in range(IN_BATCHES):
                if k < PIECES:
                    stat_piece(1, 0, 1, k)
                if k == PIECES:
                    stat_pieces_done(1)
                    stat_aggregate(1)
                take_low(0, 0, k)
            stat_deviation(1, 0, 1)
            stat_variance(1)
            bn_variance()
            stat_scale(1, 1)
            for k in range(STRIPS):
                normalise(1, 1, k)

            def step(n, m, s):
                for j in range(SLOTS):
                    if has(n, CHUNKS - 3) and j == 6:
                        stat_pieces_done(n + 2)
                    if has(n, CHUNKS - 2) and j < IN_BATCHES:
                        take_low(n + 1, 1 - s, j)
                    if has(n, CHUNKS - 3):
                        if j < 6:
                            for k in range(0 if j == 0 else j + 1, j + 2):
                                stat_piece(n + 2, m + 1, s, k)
                        if j == 6:
                            stat_aggregate(n + 2)
                        if j == 10:
                            stat_deviation(n + 2, m + 1, s)
                            stat_variance(n + 2)
                            stat_scale(n + 2, s)
                            for k in range(STRIPS):
                                normalise(n + 2, s, k)
                    if is_step(n, CHUNKS - 1) and j >= WT_AT:
                        for i in range(2):
                            weights_low(2 * (j - WT_AT) + i)
                    if is_step(n, 0) and j == 8:
                        prepare_bn()
                    if is_step(n, 1) and j == 8:
                        scale_weights(1, 0)
                    if is_step(n, CHUNKS - 4) and j == 8:
                        scale_weights(0, 2)
                    if is_step(n, CHUNKS - 3) and j == 8:
                        scale_weights(1, 2)
                    if is_step(n, CHUNKS - 2):
                        if j % 2 == 0 and j < 10:
                            transform_weights(0, j // 2)
                        if j == 10:
                            dve.wait_ge(t_full[(IN_BATCHES - 1) % 2], CHUNKS * (IN_BATCHES // 2))
                            for part in range(5):
                                transform_weights(1, part)
                            assert done == WEIGHT_STEPS
                if is_step(n, 0):
                    scale_weights(0, 0)
                if is_step(n, 1):
                    scale_weights(0, 1)
                if is_step(n, CHUNKS - 4):
                    scale_weights(1, 1)

            chunks(dve, step)
            for i in range(2):
                dve.wait_ge(wt_full[i], len(BATCHES) // 2)
            dve.wait_ge(mem.first_loaded[0], 32)
            for c in range(CT):
                nc.vector.tensor_scalar(mem.xn[c][:, 1:X_ROWS + 1, 1:W + 1], mem.X[0][:, c], mem.stp[0][:, c, 1:2],
                                        mem.stp[0][:, c, 0:1], ALU.mult, ALU.add).then_inc(mem.xn_ready[c], 1)
            for k in range(STRIPS):
                if k == 0:
                    dve.wait_ge(packed, (CHUNKS - 1) * STRIPS)
                    dve.wait_ge(o_stored[1], (CHUNKS // 2 - 1) * 16)
                dve.wait_ge(bk_free, (CHUNKS - 1) * OUT_BATCHES + batch_of[k] + 1)
                at = k * STRIP_PITCH
                nc.vector.tensor_copy(Oc[1].rearrange("p (y x) -> p y x", x=W)[:, :, k * SW:(k + 1) * SW],
                                      O[:, at:at + H * PITCH].rearrange("p (y x) -> p y x", x=PITCH)[:, :, 0:SW]
                                      ).then_inc(last_packed, 1)


def dense(nc, sb, sem, bank, mem, x3, dw_d, st_d, out3):
    ctx = ExitStack()
    with ctx:
        wt, stp = mem.wt, mem.stp
        dw_scale, scale1, bias1, fold3, bias3 = mem.dw_scale, mem.scale1, mem.bias1, mem.fold3, mem.bias3
        X = mem.X
        xn, xn_ready = mem.xn, mem.xn_ready
        at, tmp, small = mem.mid_used, [], []
        for i in range(4):
            t, at = view(mem.mid, at, [QUADS, WPAD])
            tmp.append(t)
        for i in range(6):
            t, at = view(mem.mid, at, [QUADS, W])
            small.append(t)
        at, dwt, xr, y, rep, U, Uf = 0, [], [], [], [], [], []
        for tiles, shape, dt in ((dwt, [NT], F32), (xr, [NT], F32), (y, [QUADS, 4, W], F32), (rep, [NT], F32),
                                 (U, [2, CT, KW, QUADS, WPAD], F16), (Uf, [KW, QUADS, WPAD], F32),
                                 (small, [QUADS, W], F32)):
            for c in range(CT):
                t, at = view(mem.high, at, shape, dt)
                tiles.append(t)
        first = [small[0:2], small[2:4]]
        sums, diffs = small[4:6], small[6:8]

        pad_zero = mem.pad_zero
        x_loaded = [sem(f"x_loaded{h}") for h in range(2)]
        t_ready = sem("transform_sums")
        u_ready = [sem(f"u_ready{c}") for c in range(CT)]
        u_high = [sem(f"u_high{c}") for c in range(CT)]
        u_low = [sem(f"u_low{c}") for c in range(CT)]
        full = [sem(f"product_full{k}") for k in range(KW)]
        free = [sem(f"product_free{k}") for k in range(KW - 1)]
        y_part = [sem(f"y_part{c}") for c in range(CT)]
        y_ready = [sem(f"y_ready{c}") for c in range(CT)]
        rep_ready = [sem(f"rep_ready{c}") for c in range(CT)]
        z_ready = [sem(f"z_ready{c}") for c in range(CT)]
        f_ready = [sem(f"f_ready{c}") for c in range(CT)]
        last_first, last_added = sem("last_tile_first_activation"), sem("last_tile_depthwise_added")
        last_activated, last_ready = sem("last_tile_activated"), sem("last_tile_ready")
        sum_ready = [sem(f"sum_ready{c}") for c in range(CT)]
        out_stored = [sem(f"out_stored{c}") for c in range(CT)]
        dwt_loaded = [sem(f"dwt_loaded{c}") for c in range(CT)]
        xr_loaded = [sem(f"xr_loaded{c}") for c in range(CT)]

        ORDER = (1, 2, 3, 4, 0, 5)
        HALVES = 2
        PER = KW // HALVES
        LAST_PARTS = (slice(0, NT // 2), slice(NT // 2, NT))
        T_STEPS = 6

        def slot_bank(g, i):
            return bank[(g * KW + i) % 8]

        def images(eng, image):
            image(0, True)
            with eng.Fori(1, B - 1) as b:
                image(b, True)
            image(B - 1, False)

        def previous(b, h, c):
            if c == 1:
                return b * 2 + h, h, b, 0
            if isinstance(b, int) and b == 0 and h == 0:
                return None
            return b * 2 + h - 1, 1 - h, (b if h else b - 1), 1

        block = ctx.enter_context(nc.Block())

        @block.sync
        def _(sp):
            def load_x(b, h):
                rows, stats = half_image(x3, st_d, b, h)
                sp.dma_start(X[h].rearrange("p k y x -> p k (y x)"), rows).then_inc(x_loaded[h], 16)
                sp.dma_start(stp[h][:], stats).then_inc(x_loaded[h], 16)

            def load_tile(b, h, c):
                k = b * 2 + h
                wait(sp, z_ready[c], k)
                src = dw_d[bass.ds(b, 1), c * P:(c + 1) * P, h * NT:(h + 1) * NT]
                sp.dma_start(dwt[c][:], src.rearrange("a p q -> p (a q)")).then_inc(dwt_loaded[c], 16)
                wait(sp, sum_ready[c], k)
                src = x3[bass.ds(b, 1), c * P:(c + 1) * P, h * NT:(h + 1) * NT]
                sp.dma_start(xr[c][:], src.rearrange("a p q -> p (a q)")).then_inc(xr_loaded[c], 16)

            def store(k, h, b, c):
                sp.wait_ge(sum_ready[c], k + 1)
                dst = out3[bass.ds(b, 1), c * P:(c + 1) * P, h * NT:(h + 1) * NT]
                sp.dma_start(dst.rearrange("a p q -> p (a q)"), rep[c][:]).then_inc(out_stored[c], 16)

            def image(b, more):
                for h in range(2):
                    if more:
                        for c in range(CT):
                            sp.wait_ge(xn_ready[c], b * 2 + h + 1)
                        load_x(b + 1, h)
                    for c in range(CT):
                        load_tile(b, h, c)
                        if before := previous(b, h, c):
                            store(*before)
            for s in range(2):
                sp.wait_ge(mem.o_stored[s], 16 * CHUNKS // 2)
            images(sp, image)
            for i, part in enumerate(LAST_PARTS):
                sp.wait_ge(last_ready, i + 1)
                dst = out3[B - 1:B, P:C, NT + part.start:NT + part.stop]
                sp.dma_start(dst.rearrange("a p q -> p (a q)"), rep[1][:, part]).then_inc(out_stored[1], 16)
            sp.wait_ge(out_stored[0], 16 * 2 * B)
            sp.wait_ge(out_stored[1], 16 * (2 * B - 1 + len(LAST_PARTS)))

        @block.gpsimd
        def _(pool):
            def add_residual(k, h, b, c):
                pool.wait_ge(f_ready[c], k + 1)
                pool.wait_ge(xr_loaded[c], k * 16 + 16)
                nc.gpsimd.tensor_tensor(rep[c][:], rep[c][:], xr[c][:], ALU.add).then_inc(sum_ready[c], 1)


            def image(b, more):
                for h in range(2):
                    for c in range(CT):
                        if before := previous(b, h, c):
                            add_residual(*before)
            images(pool, image)

        @block.tensor
        def _(pe):
            def image(b, more):
                for h in range(2):
                    start = isinstance(b, int) and b == 0 and h == 0
                    for c in range(CT):
                        pe.wait_ge(u_low[c], 1 if start else (b * 2 + h + 1) * HALVES)
                    for c in range(CT):
                        g = h * CT + c
                        for i, k in enumerate(ORDER):
                            if start and c == 0 and i == 2:
                                for ci in range(CT):
                                    pe.wait_ge(u_low[ci], HALVES)
                            j, back = (i - 2, 1) if i >= 2 else (i + 4, 2)
                            if j == KW - 1:
                                wait(pe, y_ready[(g - back) % CT], b * 2 + (g - back) // CT + 1)
                            else:
                                wait(pe, free[ORDER[j]], b * 4 + g - back + 1)
                            acc = slot_bank(g, i)[:, 0:N3]
                            n = 0
                            for ci in range(CT):
                                for dx in range(3):
                                    for zw, zx in ((0, 0), (0, 1), (1, 0)):
                                        last = nc.tensor.matmul(
                                            acc, wt[:, ci, k, dx, zw, c * P:(c + 1) * P],
                                            U[h][:, zx, ci, k, :, dx:dx + W],
                                            start=(n == 0), stop=(n == 9 * CT - 1))
                                        n += 1
                            last.then_inc(full[k], 1)
            images(pe, image)

        @block.scalar
        def _(act):
            def normalise(b, h, c):
                if c == 0:
                    first = isinstance(b, int) and b == 0
                    act.wait_ge(mem.first_loaded[h] if first else x_loaded[h], 32 if first else b * 32)
                wait(act, u_ready[c], (b * 2 + h) * HALVES)
                nc.scalar.activation(xn[c][:, 1:X_ROWS + 1, 1:W + 1], X[h][:, c], ACT.Identity,
                                     bias=stp[h][:, c, 0:1], scale=stp[h][:, c, 1:2]).then_inc(xn_ready[c], 1)

            def take_high(k, h, c, half):
                act.wait_ge(u_ready[c], k * HALVES + half + 1)
                wait(act, full[ORDER[-1]], k * CT - CT)
                ks = slice(half * PER, (half + 1) * PER)
                nc.scalar.copy(U[h][:, 0, c, ks].rearrange("p k y x -> p (k y x)"),
                               Uf[c][:, ks].rearrange("p k y x -> p (k y x)")).then_inc(u_high[c], 1)

            def take_product(b, h, c, i):
                k = ORDER[i]
                act.wait_ge(full[k], b * 4 + h * CT + c + 1)
                wait(act, y_ready[c], b * 2 + h)
                nc.scalar.copy(first[c][i // 2][:].rearrange("p y x -> p (y x)"),
                               slot_bank(h * CT + c, i)[:, 0:N3]).then_inc(free[k], 1)

            def activate_first(k, h, b, c):
                act.wait_ge(y_ready[c], k + 1)
                wait(act, out_stored[c], k * 16)
                nc.scalar.activation(rep[c][:], y[c][:].rearrange("p q r x -> p (q r x)"), ACT.Silu,
                                     bias=bias1[:, c:c + 1], scale=scale1[:, c:c + 1]).then_inc(rep_ready[c], 1)

            def activate_last(k, h, b, c):
                act.wait_ge(z_ready[c], k + 1)
                nc.scalar.activation(rep[c][:], rep[c][:], ACT.Silu, bias=bias3[:, c:c + 1],
                                     scale=fold3[:, c:c + 1]).then_inc(f_ready[c], 1)

            for half in range(HALVES):
                for c in range(CT):
                    take_high(0, 0, c, half)
            for c in range(CT):
                normalise(0, 1, c)
            def image(b, more):
                for h in range(2):
                    for c in range(CT):
                        before = previous(b, h, c)
                        if before:
                            activate_first(*before)
                        take_product(b, h, c, 0)
                        if more or h == 0:
                            take_high(b * 2 + h + 1, 1 - h, c, 0)
                        if before:
                            activate_last(*before)
                        take_product(b, h, c, 2)
                        if more or h == 0:
                            take_high(b * 2 + h + 1, 1 - h, c, 1)
                        if more:
                            normalise(b + 1, h, c)
            images(act, image)
            act.wait_ge(y_ready[1], 2 * B)
            act.wait_ge(out_stored[1], (2 * B - 1) * 16)
            for part in LAST_PARTS:
                nc.scalar.activation(rep[1][:, part], y[1].rearrange("p q r x -> p (q r x)")[:, part], ACT.Silu,
                                     bias=bias1[:, 1:2], scale=scale1[:, 1:2]).then_inc(last_first, 1)
            for i, part in enumerate(LAST_PARTS):
                act.wait_ge(last_added, i + 1)
                nc.scalar.activation(rep[1][:, part], rep[1][:, part], ACT.Silu, bias=bias3[:, 1:2],
                                     scale=fold3[:, 1:2]).then_inc(last_activated, 1)

        @block.vector
        def _(dve):
            def transform(k, h, c, part, ahead=False):
                d = [xn[c][:, h + j:h + j + 4 * QUADS - 3:4, :] for j in range(6)]
                t = [tmp[i][:] for i in range(4)]
                u = [Uf[c][:, j] for j in range(KW)]
                n = c * 3 + part * 6 if ahead else (k * CT + c) * T_STEPS + part * 3
                stt = nc.vector.scalar_tensor_tensor
                if part == 0:
                    dve.wait_ge(xn_ready[c], k + 1)
                    wait(dve, u_low[c], k * HALVES)
                    wait(dve, u_ready[1 - c], c if ahead else (k + c) * HALVES)
                    stt(t[0], d[2], -4.0, d[4], ALU.mult, ALU.add).then_inc(t_ready, 1)
                    stt(t[1], d[1], -4.0, d[3], ALU.mult, ALU.add).then_inc(t_ready, 1)
                    stt(t[2], d[2], -5.0, d[4], ALU.mult, ALU.add).then_inc(t_ready, 1)
                    dve.wait_ge(t_ready, n + 2)
                    nc.vector.tensor_tensor(u[1], t[0], t[1], ALU.add)
                    nc.vector.tensor_tensor(u[2], t[0], t[1], ALU.subtract)
                    dve.wait_ge(t_ready, n + 3)
                    stt(u[0], d[0], 4.0, t[2], ALU.mult, ALU.add).then_inc(u_ready[c], 1)
                else:
                    if ahead:
                        dve.wait_ge(u_ready[1 - c], 1 + c)
                    stt(t[3], d[3], -5.0, d[5], ALU.mult, ALU.add).then_inc(t_ready, 1)
                    if not ahead:
                        dve.wait_ge(u_ready[c], k * HALVES + 1)
                    nc.vector.tensor_tensor(t[0], d[4], d[2], ALU.subtract).then_inc(t_ready, 1)
                    nc.vector.tensor_tensor(t[1], d[3], d[1], ALU.subtract).then_inc(t_ready, 1)
                    dve.wait_ge(t_ready, n + 3)
                    stt(u[3], t[1], 2.0, t[0], ALU.mult, ALU.add)
                    stt(u[4], t[1], -2.0, t[0], ALU.mult, ALU.add)
                    stt(u[5], d[1], 4.0, t[3], ALU.mult, ALU.add).then_inc(u_ready[c], 1)

            def take_low(k, h, c, half):
                dve.wait_ge(u_high[c], k * HALVES + half + 1)
                ks = slice(half * PER, (half + 1) * PER)
                high, low = (U[h][:, z, c, ks].rearrange("p k y x -> p (k y x)") for z in range(2))
                nc.vector.tensor_tensor(low, Uf[c][:, ks].rearrange("p k y x -> p (k y x)"), high,
                                        ALU.subtract).then_inc(u_low[c], 1)

            def product(h, c, i):
                return slot_bank(h * CT + c, i)[:, 0:N3].rearrange("p (y x) -> p y x", x=W)

            def pair(b, h, c, i):
                g = b * 4 + h * CT + c + 1
                if i == 0 and (before := previous(b, h, c)):
                    dve.wait_ge(y_ready[1 - c], before[0] + 1)
                dve.wait_ge(free[ORDER[i]], g)
                dve.wait_ge(full[ORDER[i + 1]], g)
                a = first[c][i // 2][:]
                nc.vector.tensor_tensor(sums[i // 2][:], a, product(h, c, i + 1), ALU.add)
                nc.vector.tensor_tensor(diffs[i // 2][:], a, product(h, c, i + 1), ALU.subtract
                                        ).then_inc(free[ORDER[i + 1]], 1)

            def rows(b, h, c):
                (p, r), (q, s) = (x[:] for x in sums), (x[:] for x in diffs)
                dve.wait_ge(free[ORDER[3]], b * 4 + h * CT + c + 1)
                wait(dve, rep_ready[c], b * 2 + h)
                stt = nc.vector.scalar_tensor_tensor
                nc.vector.tensor_tensor(y[c][:, :, 0], p, r, ALU.add).then_inc(y_part[c], 1)
                stt(y[c][:, :, 3], s, 8.0, q, ALU.mult, ALU.add).then_inc(y_part[c], 1)
                stt(y[c][:, :, 1], s, 2.0, q, ALU.mult, ALU.add)
                stt(y[c][:, :, 2], r, 4.0, p, ALU.mult, ALU.add)

            def last_rows(b, h, c):
                g = b * 4 + h * CT + c + 1
                dve.wait_ge(y_part[c], (b * 2 + h) * 2 + 2)
                dve.wait_ge(full[0], g)
                nc.vector.tensor_tensor(y[c][:, :, 0], y[c][:, :, 0], product(h, c, 4), ALU.add
                                        ).then_inc(free[0], 1)
                dve.wait_ge(full[5], g)
                nc.vector.tensor_tensor(y[c][:, :, 3], y[c][:, :, 3], product(h, c, 5), ALU.add
                                        ).then_inc(y_ready[c], 1)

            def add_depthwise(k, h, b, c):
                dve.wait_ge(rep_ready[c], k + 1)
                dve.wait_ge(dwt_loaded[c], k * 16 + 16)
                nc.vector.scalar_tensor_tensor(rep[c], dwt[c], dw_scale[:, c:c + 1], rep[c], ALU.mult, ALU.add
                                               ).then_inc(z_ready[c], 1)

            dve.wait_ge(pad_zero, 2 * CT)
            for half in range(HALVES):
                for c in range(CT):
                    transform(0, 0, c, half, ahead=True)
                for c in range(CT):
                    take_low(0, 0, c, half)
            def image(b, more):
                for h in range(2):
                    for c in range(CT):
                        prepare = more or h == 0
                        k = b * 2 + h + 1
                        if prepare:
                            transform(k, 1 - h, c, 0)
                        if before := previous(b, h, c):
                            add_depthwise(*before)
                        pair(b, h, c, 0)
                        if prepare:
                            transform(k, 1 - h, c, 1)
                            take_low(k, 1 - h, c, 0)
                        pair(b, h, c, 2)
                        rows(b, h, c)
                        if prepare:
                            take_low(k, 1 - h, c, 1)
                        last_rows(b, h, c)
            images(dve, image)
            dve.wait_ge(dwt_loaded[1], 2 * B * 16)
            dve.wait_ge(xr_loaded[1], 2 * B * 16)
            for i, part in enumerate(LAST_PARTS):
                dve.wait_ge(last_first, i + 1)
                nc.vector.scalar_tensor_tensor(rep[1][:, part], dwt[1][:, part], dw_scale[:, 1:2], rep[1][:, part],
                                               ALU.mult, ALU.add).then_inc(last_added, 1)
            for i, part in enumerate(LAST_PARTS):
                dve.wait_ge(last_activated, i + 1)
                nc.vector.tensor_tensor(rep[1][:, part], rep[1][:, part], xr[1][:, part], ALU.add
                                        ).then_inc(last_ready, 1)


_NAMES = ["x"] + ["L0_conv_" + n for n in ("w3", "g1", "b1", "m1", "v1", "w1", "g2", "b2", "m2", "v2",
                                           "dw7", "dwk", "g3", "b3", "m3", "v3")]


def kernel(**inputs):
    import numpy as _np
    import concourse.bacc as _bacc
    from concourse import mybir as _mybir
    from concourse.bass_utils import run_bass_kernel_spmd as _run

    nc = _bacc.Bacc("TRN2", target_bir_lowering=False, num_devices=1)
    arrays, args = {}, []
    p = _np.arange(P)
    consts = {
        "ident": _np.eye(P, dtype=_np.float32),
        "gmat": (p[:, None] % B == p[None, :] % B).astype(_np.float32) / _np.float32(GROUP_C),
    }
    for name in _NAMES + list(consts):
        a = _np.ascontiguousarray(inputs[name] if name in inputs else consts[name])
        arrays[f"in_{name}"] = a
        args.append(nc.dram_tensor(f"in_{name}", a.shape, _mybir.dt.from_np(a.dtype), kind="ExternalInput").ap())
    args.append(nc.dram_tensor("out_0", (B, C, H, W), F32, kind="ExternalOutput").ap())
    build(nc, *args)
    r = _run(nc, [arrays], core_ids=[0])
    return r.results[0]["out_0"]
```
